# Optimizing a Trainium2 kernel written in Bass

```python
import numpy as np
import jax
import jax.numpy as jnp

def _softmax(x, axis=-1):
    return jax.nn.softmax(x, axis=axis)

def _gelu(x):
    return jax.nn.gelu(x, approximate=True)

def _silu(x):
    return jax.nn.silu(x)

def _sigmoid(x):
    return jax.nn.sigmoid(x)

def _layernorm(x, axis=-1, eps=1e-05):
    m = jnp.mean(x, axis=axis, keepdims=True)
    v = jnp.var(x, axis=axis, keepdims=True)
    return (x - m) / jnp.sqrt(v + eps)

def _scatter_add(tgt, idx, src, axis=0):
    return tgt.at[idx].add(src)

def _segment_sum(src, seg, n):
    return jax.ops.segment_sum(src, seg, n)
kernel_name = 'mk_flamingo_gated_d1_seqx_r4_84b567'

def setup_inputs(seed: int=0):
    np.random.seed(seed)
    _w = jnp.asarray

    def _rec_inputs():
        import jax
        import jax.numpy as jnp
        _rk = jax.random.key(seed)
        x = 7.22e-05 + 1 * jax.random.normal(jax.random.fold_in(_rk, 1), (32, 256, 256), jnp.float32)
        _lenS = 256 - jax.random.randint(jax.random.fold_in(_rk, 7), (32,), 0, max(1, 256 // 4) + 1, jnp.int32)
        _lenS2 = 77 - jax.random.randint(jax.random.fold_in(_rk, 8), (32,), 0, max(1, 77 // 4) + 1, jnp.int32)
        _ctx_1024P = jax.random.normal(jax.random.fold_in(_rk, 11), (32, 16, 256), jnp.float32)
        _ctx_1024c = jax.random.dirichlet(jax.random.fold_in(_rk, 511), 0.3 * jnp.ones((16,), jnp.float32), (32, 77))
        _ctx_1024t = jnp.einsum('bsk,bkd->bsd', _ctx_1024c, _ctx_1024P)
        _ctx_1024t = _ctx_1024t * jax.lax.rsqrt(jnp.mean(jnp.square(_ctx_1024t)) + 1e-12) * 0.953939
        ctx_1024 = 4.13588e-05 + 0.999923 * (_ctx_1024t + 0.3 * jax.random.normal(jax.random.fold_in(_rk, 611), (32, 77, 256), jnp.float32))
        _validS = jnp.arange(256)[None, :] < _lenS[:, None]
        _validS2 = jnp.arange(77)[None, :] < _lenS2[:, None]
        _causal = jnp.tril(jnp.ones((256, 256), dtype=bool))
        mask_BxS2_ik0 = jnp.where(jnp.broadcast_to(_validS2[:, :], (32, 77)), 0, 1).astype(jnp.int32)
        _g = jax.random.normal(jax.random.fold_in(_rk, 9001), (2, 1), jnp.float32)
        _g = jnp.sign(_g) * jnp.maximum(jnp.abs(_g), 1.0) + (_g == 0) * 1.0
        g_xattn = _g[0]
        g_ffn = _g[1]
        return (x, ctx_1024, mask_BxS2_ik0, g_xattn, g_ffn)
    x, ctx_1024, mask_BxS2_ik0, g_xattn, g_ffn = _rec_inputs()

    def _L0_xattn_setup():
        import jax, jax.numpy as jnp
        import numpy as np
        HID_DIM = 256
        N_HEADS = 16
        HEAD_DIM = HID_DIM // N_HEADS

        def _split_heads(x, B):
            return x.reshape(B, -1, N_HEADS, HEAD_DIM).transpose(0, 2, 1, 3)
        key = jax.random.key(seed)
        ks = jax.random.split(key, 12)
        B, S, D = (4, 512, HID_DIM)
        sc = 1.0 / np.sqrt(D)
        inp = {'query': jax.random.normal(ks[0], (B, S, D), jnp.float32), 'key': jax.random.normal(ks[1], (B, S, D), jnp.float32), 'value': jax.random.normal(ks[2], (B, S, D), jnp.float32), 'mask': jax.random.randint(ks[3], (B, S), 0, 2, jnp.int32), 'Wq': jax.random.normal(ks[4], (D, D), jnp.float32) * sc, 'bq': jnp.zeros((D,), jnp.float32), 'Wk': jax.random.normal(ks[5], (D, D), jnp.float32) * sc, 'bk': jnp.zeros((D,), jnp.float32), 'Wv': jax.random.normal(ks[6], (D, D), jnp.float32) * sc, 'bv': jnp.zeros((D,), jnp.float32), 'Wfc': jax.random.normal(ks[7], (D, D), jnp.float32) * sc, 'bfc': jnp.zeros((D,), jnp.float32)}
        return inp
    _L0_xattn_all = _L0_xattn_setup()
    _L0_xattn_in = {k: v for k, v in _L0_xattn_all.items() if k in ('Wq', 'bq', 'Wk', 'bk', 'Wv', 'bv', 'Wfc', 'bfc')}
    del _L0_xattn_all

    def _L0_ffn_setup():
        import jax, jax.numpy as jnp
        import numpy as np
        NUM_EXPERTS = 8
        TOP_K = 2
        key = jax.random.key(seed)
        ks = jax.random.split(key, 5)
        B, L, E, H, N = (2, 512, 256, 512, NUM_EXPERTS)
        return {'x': jax.random.normal(ks[0], (B, L, E), dtype=jnp.float32), 'gate_kernel': jax.random.normal(ks[1], (E, N), dtype=jnp.float32) / np.sqrt(E), 'w0_kernel': jax.random.normal(ks[2], (N, E, H), dtype=jnp.float32) / np.sqrt(E), 'w1_kernel': jax.random.normal(ks[3], (N, E, H), dtype=jnp.float32) / np.sqrt(E), 'wo_kernel': jax.random.normal(ks[4], (N, H, E), dtype=jnp.float32) / np.sqrt(H)}
    _L0_ffn_all = _L0_ffn_setup()
    _L0_ffn_in = {k: v for k, v in _L0_ffn_all.items() if k in ('gate_kernel', 'w0_kernel', 'w1_kernel', 'wo_kernel')}
    del _L0_ffn_all
    return {'x': x, 'ctx_1024': ctx_1024, 'mask_BxS2_ik0': mask_BxS2_ik0, 'g_xattn': g_xattn, 'g_ffn': g_ffn, 'L0_xattn_Wq': _L0_xattn_in['Wq'], 'L0_xattn_bq': _L0_xattn_in['bq'], 'L0_xattn_Wk': _L0_xattn_in['Wk'], 'L0_xattn_bk': _L0_xattn_in['bk'], 'L0_xattn_Wv': _L0_xattn_in['Wv'], 'L0_xattn_bv': _L0_xattn_in['bv'], 'L0_xattn_Wfc': _L0_xattn_in['Wfc'], 'L0_xattn_bfc': _L0_xattn_in['bfc'], 'L0_ffn_gate_kernel': _L0_ffn_in['gate_kernel'], 'L0_ffn_w0_kernel': _L0_ffn_in['w0_kernel'], 'L0_ffn_w1_kernel': _L0_ffn_in['w1_kernel'], 'L0_ffn_wo_kernel': _L0_ffn_in['wo_kernel']}

def reference(x, ctx_1024, mask_BxS2_ik0, g_xattn, g_ffn, L0_xattn_Wq, L0_xattn_bq, L0_xattn_Wk, L0_xattn_bk, L0_xattn_Wv, L0_xattn_bv, L0_xattn_Wfc, L0_xattn_bfc, L0_ffn_gate_kernel, L0_ffn_w0_kernel, L0_ffn_w1_kernel, L0_ffn_wo_kernel):
    import jax
    import jax.numpy as jnp

    def _L0_xattn_ref(query, key, value, mask, Wq, bq, Wk, bk, Wv, bv, Wfc, bfc):
        import jax, jax.numpy as jnp
        import numpy as np
        HID_DIM = 256
        N_HEADS = 16
        HEAD_DIM = HID_DIM // N_HEADS

        def _split_heads(x, B):
            return x.reshape(B, -1, N_HEADS, HEAD_DIM).transpose(0, 2, 1, 3)
        B = query.shape[0]
        Q = _split_heads(query @ Wq.T + bq, B)
        K = _split_heads(key @ Wk.T + bk, B)
        V = _split_heads(value @ Wv.T + bv, B)
        scale = jnp.sqrt(jnp.float32(HEAD_DIM))
        energy = jnp.einsum('bhqd,bhkd->bhqk', Q, K) / scale
        energy = jnp.where(mask[:, None, None, :] == 0, jnp.float32(-10000000000.0), energy)
        attention = jax.nn.softmax(energy, axis=-1)
        x = jnp.einsum('bhqk,bhkd->bhqd', attention, V)
        x = x.transpose(0, 2, 1, 3).reshape(B, -1, HID_DIM)
        return x @ Wfc.T + bfc

    def _L0_ffn_ref(x, gate_kernel, w0_kernel, w1_kernel, wo_kernel):
        import jax, jax.numpy as jnp
        import numpy as np
        NUM_EXPERTS = 8
        TOP_K = 2
        B, L, E = x.shape
        gate_logits = jnp.einsum('ble,en->bln', x, gate_kernel)
        top_k_weights, top_k_indices = jax.lax.top_k(gate_logits, TOP_K)
        softmax_probs = jax.nn.softmax(top_k_weights.astype(jnp.float32), axis=-1)
        weights = jnp.zeros_like(gate_logits)
        b_idx = jnp.arange(B)[:, None, None]
        l_idx = jnp.arange(L)[:, None]
        weights = weights.at[b_idx, l_idx, top_k_indices].set(softmax_probs)
        layer_w0 = jnp.einsum('ble,neh->blnh', x, w0_kernel)
        layer_w1 = jnp.einsum('ble,neh->blnh', x, w1_kernel)
        layer_mult = jax.nn.silu(layer_w0) * layer_w1
        intermediate = jnp.einsum('blnh,nhe->blne', layer_mult, wo_kernel)
        output = jnp.einsum('blne,bln->ble', intermediate, weights)
        return output
    x = x + jnp.tanh(g_xattn[0]) * _L0_xattn_ref(_layernorm(x, axis=-1), ctx_1024, ctx_1024, mask_BxS2_ik0, L0_xattn_Wq, L0_xattn_bq, L0_xattn_Wk, L0_xattn_bk, L0_xattn_Wv, L0_xattn_bv, L0_xattn_Wfc, L0_xattn_bfc)
    x = x + jnp.tanh(g_ffn[0]) * _L0_ffn_ref(_layernorm(x, axis=-1), L0_ffn_gate_kernel, L0_ffn_w0_kernel, L0_ffn_w1_kernel, L0_ffn_wo_kernel)
    return x

_drawn_inputs = setup_inputs


def setup_inputs(seed=0):
    import zlib

    import numpy as np

    out = dict(_drawn_inputs(seed))
    spreads = {'L0_xattn_bq': (0.0, 0.1),
     'L0_xattn_bk': (0.0, 0.1),
     'L0_xattn_bv': (0.0, 0.1),
     'L0_xattn_bfc': (0.0, 0.1)}
    factors = {}
    for name, (base, spread) in spreads.items():
        noise = np.random.default_rng([zlib.crc32(name.encode()), seed]).standard_normal(out[name].shape)
        drawn = base * np.exp(spread * noise) if base else spread * noise
        out[name] = jnp.asarray(drawn.astype(out[name].dtype))
    for name, factor in factors.items():
        out[name] = (out[name] * factor).astype(out[name].dtype)
    return out
```

```python
from contextlib import ExitStack

import concourse.bass as bass
from concourse import mybir

F32 = mybir.dt.float32
BF16 = mybir.dt.bfloat16
I32 = mybir.dt.int32
U32 = mybir.dt.uint32
ALU = mybir.AluOpType
ACT = mybir.ActivationFunctionType
AX_X = mybir.AxisListType.X

P = 128
EPS = 1e-5
MASKED = -1e10
TOP_K = 2
ROW = 2


def flamingo_gated_layer(nc, x, ctx_in, mask, g_xattn, g_ffn, Wq, bq, Wk, bk, Wv, bv, Wfc, bfc,
                         gate_kernel, w0, w1, wo, out):
    B, S, D = x.shape
    K2 = ctx_in.shape[1]
    HD = 16
    H = D // HD
    QT = S // P
    NT = B * QT
    DC = D // P
    E, _, F = w0.shape
    FC = F // P
    scale = float(HD) ** -0.5
    assert QT == 2 and DC == 2 and B % 4 == 0

    PAIR = 2 * K2
    HK = H * K2
    CH = -(-HK // P)
    first_head = [min(P * c // K2, H - 3) for c in range(CH)]
    VW = HD + 1
    T_GROUPS = [(0, 4), (4, 8), (8, CH)]

    REGION = NT + 1
    MOE_T = NT * TOP_K + E
    SPARE = MOE_T - NT * TOP_K + 1
    RW = D + ROW
    routed = nc.dram_tensor("routed_rows", [(E * REGION + SPARE) * P, RW], F32, kind="Internal").ap()

    x_t = x.rearrange("b (t p) d -> b p t d", p=P)
    gx = g_xattn.rearrange("(o a) -> o a", o=1)
    gf = g_ffn.rearrange("(o a) -> o a", o=1)

    with ExitStack() as ctx:
        def sb(name, shape, dt=F32):
            return ctx.enter_context(nc.sbuf_tensor(name, shape, dt))

        def ps(name, shape, dt=F32):
            return ctx.enter_context(nc.psum_tensor(name, shape, dt))

        def sem(name):
            return ctx.enter_context(nc.semaphore(name))

        w0_sb = sb("w0_sb", [P, E, DC, F])
        w1_sb = sb("w1_sb", [P, E, DC, F])
        wo_sb = sb("wo_sb", [P, E, FC, D])
        wT = {n: sb(f"{n}T", [P, DC, D]) for n in ("wq", "wk", "wv", "wfc")}
        gate_sb = sb("gate_sb", [P, DC, E])
        bias = sb("bias", [P, 3, DC])
        bfc_rows = sb("bfc_rows", [P, D])
        gates = sb("gates", [P, 2])
        tanhg = sb("tanhg", [P, 2])
        ident = sb("ident", [P, P])
        upper = sb("upper", [P, P], BF16)
        ones = sb("ones", [P, P], BF16)
        valid = sb("valid", [P, B * K2], BF16)
        masked = sb("masked", [P, B * K2], BF16)
        parity = sb("parity", [P, 2])
        parity_i = sb("parity_i", [P, 2], I32)
        head_i = sb("head_i", [P, CH, H], I32)
        head_f = sb("head_f", [P, CH, H])
        head_lt = sb("head_lt", [P, CH, H])
        head_of = sb("head_of", [P, CH, 3])
        token_id = sb("token_id", [P, NT])
        token_i = sb("token_i", [P, NT], I32)
        expert_i = sb("expert_i", [P, 2, E], I32)
        expert_f = sb("expert_f", [P, 2, E])
        half_neg = sb("half_neg", [P, 2])
        region0 = sb("region0", [P, E])
        pad_rows = sb("pad_rows", [P, RW])
        pad_i = sb("pad_i", [P, 1], I32)

        xb = sb("xb", [P, 2, QT, D])
        xg = sb("xg", [P, 2, QT, D])
        cb = sb("cb", [K2, 2, D])
        xn = sb("xn", [P, QT, D])
        xnT = sb("xnT", [P, DC, S])
        ctxT = sb("ctxT", [P, DC, 3, K2])
        qT = sb("qT", [P, 2, 2, S])
        kbd = sb("kbd", [P, 2, 2, 2, K2])
        kmask = sb("kmask", [P, 2, 2, K2])
        mrow = sb("mrow", [P, 2, 4, K2], BF16)
        vbd = sb("vbd", [P, 2, CH, 3, VW])
        prob = sb("prob", [P, 2, CH * P])
        probT = sb("probT", [P, CH, P])
        mx = sb("mx", [P, 2, H])
        rden = sb("rden", [P, H])
        on = sb("on", [P, D])
        onT = sb("onT", [P, DC, P])
        x1 = sb("x1", [P, 2, D])
        st1 = sb("st1", [P, QT, 6])
        mv1 = sb("mv1", [P, QT, 2])
        ve1 = sb("ve1", [P, QT])
        rs1 = sb("rs1", [P, QT])
        st2 = sb("st2", [P, 6])
        mv2 = sb("mv2", [P, 2])
        ve2 = sb("ve2", [P, 1])
        rs2 = sb("rs2", [P, 1])
        rows = sb("rows", [P, 4, TOP_K, RW])
        xn2T = sb("xn2T", [P, DC, P])
        logit = sb("logit", [P, E])
        top = sb("top", [P, 8])
        topi = sb("topi", [P, 8], U32)
        topf = sb("topf", [P, TOP_K])
        chosen = sb("chosen", [P, TOP_K, E])
        chosen_any = sb("chosen_any", [P, E], BF16)
        gap = sb("gap", [P, 1])
        egap = sb("egap", [P, 1])
        wsum = sb("wsum", [P, 1])
        wrec = sb("wrec", [P, 1])
        pos = sb("pos", [P, E])
        base = sb("base", [P, E])
        picked = sb("picked", [P, TOP_K, E])
        slotf = sb("slotf", [P, TOP_K])
        slot = sb("slot", [P, 4, TOP_K], I32)
        base_i = sb("base_i", [P, E], I32)
        cnt_f = sb("cnt_f", [P, E])
        cnt_i = sb("cnt_i", [P, E], I32)
        nt_i = sb("nt_i", [P, E], I32)
        nt_f = sb("nt_f", [P, E])
        one_e = sb("one_e", [P, E])
        tend = sb("tend", [P, E])
        skip = sb("skip", [P, E])
        tile_i = sb("tile_i", [P, MOE_T], I32)
        tile_f = sb("tile_f", [P, MOE_T])
        past = sb("past", [P, MOE_T, E])
        texp = sb("texp", [P, MOE_T])
        texp2 = sb("texp2", [P, MOE_T])
        tblk = sb("tblk", [P, MOE_T])
        texp_i = sb("texp_i", [P, MOE_T], I32)
        tblk_i = sb("tblk_i", [P, MOE_T], I32)
        mask_sb = prob[:].rearrange("p t n -> p (t n)").bitcast(I32)[:, 0:B * K2]

        et = sb("et", [P, 4, RW])
        etT = sb("etT", [P, 2, DC, P])
        hbuf = sb("hbuf", [P, 4, F])
        hs, hg = hbuf[:, 0:2], hbuf[:, 2:4]
        raw = hbuf[:].rearrange("p n (c d) -> p n c d", c=DC)
        hgT = sb("hgT", [P, 2, FC, P])
        ey = sb("ey", [P, 2, D])
        eid = sb("eid", [P, 4], I32)

        psS = ps("psS", [P, 4, 512])
        psT = ps("psT", [P, 512])
        psG = ps("psG", [P, 512])
        psA = ps("psA", [P, 512])
        psB = ps("psB", [P, 512])

        raw_in, const_in, mask_in, gates_in = sem("raw_in"), sem("const_in"), sem("mask_in"), sem("gates_in")
        gate_in, moe_in, x_in, ctx_in_s = sem("gate_in"), sem("moe_in"), [sem("x_in0"), sem("x_in1")], [sem("ctx_in0"), sem("ctx_in1")]
        x1_out, pad_out, scattered = [sem("x1_out0"), sem("x1_out1")], sem("pad_out"), [sem(f"scattered{j}") for j in range(4)]
        iota_done, ident_done, dv_const, sel_done = sem("iota_done"), sem("ident_done"), sem("dv_const"), sem("sel_done")
        wT_ps, wT_sb, tanh_done, valid_done = sem("wT_ps"), sem("wT_sb"), sem("tanh_done"), sem("valid_done")
        stat1, mvar1, eps1, rstd1, xn_done = sem("stat1"), sem("mvar1"), sem("eps1"), sem("rstd1"), sem("xn_done")
        xg_done, kmask_done, mrow_done = sem("xg_done"), sem("kmask_done"), sem("mrow_done")
        ctxT_ps, ctxT_sb, xT_ps, xT_sb = sem("ctxT_ps"), sem("ctxT_sb"), sem("xT_ps"), sem("xT_sb")
        k_ps, k_sb, q_ps, q_sb, v_ps, v_sb = (sem(n) for n in ("k_ps", "k_sb", "q_ps", "q_sb", "v_ps", "v_sb"))
        s_ps, s_max, s_sub, p_done = sem("s_ps"), sem("s_max"), sem("s_sub"), sem("p_done")
        t_ps, t_sb, o_ps, o_rec, o_sb = sem("t_ps"), sem("t_sb"), sem("o_ps"), sem("o_rec"), sem("o_sb")
        oT_ps, oT_sb, y_ps, x1_done = sem("oT_ps"), sem("oT_sb"), sem("y_ps"), sem("x1_done")
        stat2, mvar2, eps2, rstd2, xn2_done = sem("stat2"), sem("mvar2"), sem("eps2"), sem("rstd2"), sem("xn2_done")
        n2T_ps, n2T_sb, g_ps, r_ps = sem("n2T_ps"), sem("n2T_sb"), sem("g_ps"), sem("r_ps")
        l_cp, l_max, l_idx, l_idf, l_oh, l_any, gap_done = (
            sem(n) for n in ("l_cp", "l_max", "l_idx", "l_idf", "l_oh", "l_any", "gap_done"))
        egap_done, w_sum, w_rec, w_one, w_done = (sem(n) for n in ("egap_done", "w_sum", "w_rec", "w_one", "w_done"))
        pos_done, base_done, pick_done, slotf_done, slot_done = (
            sem(n) for n in ("pos_done", "base_done", "pick_done", "slotf_done", "slot_done"))
        row_copy = sem("row_copy")
        passed = {e.engine: sem(f"passed{n}") for n, e in enumerate((nc.sync, nc.gpsimd, nc.vector))}
        tab, tab_done = sem("tab"), sem("tab_done")
        et_in, etT_ps, etT_sb, h0_ps, h1_ps = [sem(f"et_in{j}") for j in range(4)], sem("etT_ps"), sem("etT_sb"), sem("h0_ps"), sem("h1_ps")
        hs_done, hg_done, hgT_ps, hgT_sb, ey_ps, ey_done, eid_done, added = (
            sem(n) for n in ("hs_done", "hg_done", "hgT_ps", "hgT_sb", "ey_ps", "ey_done", "eid_done", "added"))

        CONST_LOADS = 1 + 3 * 2
        N_IOTA, N_SEL = 8, 3
        UNR = 2
        LOOPS = B // UNR
        PEELED = 2

        def batches(eng, body):
            for b in range(PEELED * UNR):
                body(b, b % UNR, b // UNR)
            with eng.Fori(PEELED, LOOPS - 1) as it:
                for u in range(UNR):
                    body(it * UNR + u, u, it)
            for u in range(UNR):
                body(B - UNR + u, u, LOOPS - 1)

        def tiles(eng, body, n=MOE_T, unroll=4):
            for u in range(unroll):
                body(u, u, 0)
            with eng.Fori(1, n // unroll - 1) as it:
                for u in range(unroll):
                    body(it * unroll + u, u, it)
            for u in range(unroll):
                body(n - unroll + u, u, n // unroll - 1)

        def known(v, least):
            return not isinstance(v, int) or v >= least

        def below(v, end):
            return not isinstance(v, int) or v < end

        def after(eng, *waits):
            for done, v in waits:
                eng.wait_ge(done, v)
            if waits:
                eng.sem_inc(passed[eng.engine], 1)

        block = ctx.enter_context(nc.Block())

        @block.sync
        def _(sp):
            def load_batch(b, u):
                sp.dma_start(xb[:, u], x_t[b] if isinstance(b, int) else x_t[bass.ds(b, 1)].rearrange("o p t d -> p (o t) d")).then_inc(x_in[u], 16)
                sp.dma_start(cb[:, u], ctx_in[b] if isinstance(b, int) else ctx_in[bass.ds(b, 1)].rearrange("o k d -> k (o d)")).then_inc(ctx_in_s[u], 16)

            sp.dma_start(xb[:, 0], x_t[0]).then_inc(x_in[0], 16)
            for n, w in enumerate((Wq, Wk)):
                wv = w.rearrange("(r a q) d -> a r q d", a=2, r=4)
                for a in range(2):
                    for r in range(4):
                        sp.dma_start(raw[32 * r:32 * r + 32, n, a], wv[a, r]).then_inc(raw_in, 16)
            sp.dma_start(cb[:, 0], ctx_in[0]).then_inc(ctx_in_s[0], 16)
            for n, w in ((2, Wv), (3, Wfc)):
                sp.dma_start(raw[:, n], w.rearrange("(c p) d -> p c d", p=P)).then_inc(raw_in, 16)
            load_batch(1, 1)
            sp.dma_start(mask_sb, mask.rearrange("b k -> (b k)").rearrange("(o n) -> o n", o=1).to_broadcast([P, B * K2])).then_inc(mask_in, 16)
            sp.dma_start(gate_sb[:], gate_kernel.rearrange("(c p) e -> p c e", p=P)).then_inc(gate_in, 16)
            sp.wait_ge(dv_const, 1)
            sp.dma_start(out[NT * P:NT * P + P, :], pad_rows[:, 0:D]).then_inc(pad_out, 16)
            for e in range(E):
                sp.dma_start(w0_sb[:, e], w0[e].rearrange("(c p) f -> p c f", p=P)).then_inc(moe_in, 16)
                sp.dma_start(w1_sb[:, e], w1[e].rearrange("(c p) f -> p c f", p=P)).then_inc(moe_in, 16)
                sp.dma_start(wo_sb[:, e], wo[e].rearrange("(c p) d -> p c d", p=P)).then_inc(moe_in, 16)

            def store_x1(i, slot_):
                sp.wait_ge(x1_done, i + 1)
                dst = out[i * P:(i + 1) * P, :] if isinstance(i, int) else out[bass.ds(i * P, P), :]
                sp.dma_start(dst, x1[:, slot_]).then_inc(x1_out[slot_], 16)

            def batch(b, u, n):
                if known(b, 1):
                    store_x1(b * QT - 1, 1)
                if below(b, B - 2):
                    after(sp, (xn_done, b + 1))
                    after(sp, (xg_done, QT * (b + 1)))
                    after(sp, (ctxT_ps, b + 1))
                    load_batch(b + 2, u)
                store_x1(b * QT, 0)

            batches(sp, batch)
            store_x1(NT - 1, 1)

            sp.wait_ge(tab_done, 1)
            for done in scattered:
                sp.wait_ge(done, 32 * NT // 4)
            for e in range(E):
                r = sp.value_load(base_i[0:1, e:e + 1], min_val=e * REGION * P, max_val=e * REGION * P + NT * P)
                sp.dma_start(routed[bass.ds(r, P), :], pad_rows[:]).then_inc(pad_out, 16)
            for s in range(SPARE):
                t0 = (E * REGION + s) * P
                sp.dma_start(routed[t0:t0 + P, :], pad_rows[:]).then_inc(pad_out, 16)
            sp.wait_ge(pad_out, 16 * (1 + E + SPARE))
            for done in x1_out:
                sp.wait_ge(done, 16 * B)

            def load_rows(t, u, q):
                if known(t, 4):
                    after(sp, (ey_done, t - 3), (eid_done, t - 3))
                r = sp.value_load(tblk_i[0:1, bass.ds(t, 1)], min_val=0, max_val=E * REGION + SPARE - 1)
                sp.dma_start(et[:, u], routed[bass.ds(r * P, P), :]).then_inc(et_in[u], 16)

            tiles(sp, load_rows)

        @block.gpsimd
        def _(gp):
            gp.dma_start(gates[:, 0:1], gx.to_broadcast([P, 1])).then_inc(gates_in, 16)
            gp.dma_start(gates[:, 1:2], gf.to_broadcast([P, 1])).then_inc(gates_in, 16)
            gp.dma_start(bfc_rows[:], bfc.rearrange("(o d) -> o d", o=1).to_broadcast([P, D])).then_inc(const_in, 16)
            with nc.allow_non_contiguous_dma(reason="biases, one word a partition"):
                for n, v in enumerate((bq, bk)):
                    for a in range(2):
                        gp.dma_start(bias[:, n, a:a + 1], v.rearrange("(r a q) -> a r q", a=2, r=4)[a].rearrange("r (q o) -> r q o", o=1)).then_inc(const_in, 16)
                for a in range(2):
                    gp.dma_start(bias[:, 2, a:a + 1], bv[a * P:(a + 1) * P].rearrange("(q o) -> q o", o=1)).then_inc(const_in, 16)
            gp.iota(head_i[:], [[P, CH], [-K2, H]], base=0, channel_multiplier=1).then_inc(iota_done, 1)
            gp.iota(parity_i[:], [[0, 2]], base=0, channel_multiplier=1).then_inc(iota_done, 1)
            gp.iota(token_i[:], [[P, NT]], base=0, channel_multiplier=1).then_inc(iota_done, 1)
            gp.iota(expert_i[:], [[0, 2], [1, E]], base=0, channel_multiplier=0).then_inc(iota_done, 1)
            gp.iota(tile_i[:], [[1, MOE_T]], base=0, channel_multiplier=0).then_inc(iota_done, 1)
            gp.iota(pad_i[:], [[0, 1]], base=NT * P, channel_multiplier=1).then_inc(iota_done, 1)
            gp.memset(ident[:], 0.0).then_inc(iota_done, 1)
            gp.memset(upper[:], 1.0).then_inc(iota_done, 1)
            gp.wait_ge(iota_done, N_IOTA)
            gp.affine_select(out=ident[:], in_=ident[:], compare_op=ALU.not_equal, fill=1.0, base=0,
                             pattern=[[-1, P]], channel_multiplier=1).then_inc(ident_done, 1)
            gp.affine_select(out=upper[:], in_=upper[:], compare_op=ALU.is_gt, fill=0.0, base=0,
                             pattern=[[1, P]], channel_multiplier=-1).then_inc(ident_done, 1)

            def rstd_1(b):
                after(gp, (mvar1, QT * (b + 1)))
                gp.tensor_scalar(ve1[:], mv1[:, :, 1], EPS, 1.0, ALU.add, ALU.mult).then_inc(eps1, 1)
                gp.wait_ge(eps1, b + 1)
                gp.tensor_tensor(rs1[:], ve1[:], half_neg[:], ALU.pow).then_inc(rstd1, 1)

            def masks(b, u):
                after(gp, *([(s_ps, QT * (b - 1))] if known(b, 2) else []))
                gp.tensor_copy(mrow[:, u], masked[:, bass.ds(b * K2, K2)].rearrange("p (o k) -> p o k", o=1).to_broadcast([P, 4, K2])).then_inc(mrow_done, 1)

            def residual(b, u, n):
                gp.wait_ge(x_in[u], 16 * (n + 1))
                if known(b, 2):
                    gp.wait_ge(x1_done, QT * (b - 1))
                for t in range(QT):
                    gp.tensor_tensor(xg[:, u, t], xb[:, u, t], bfc_rows[:], ALU.add).then_inc(xg_done, 1)

            gp.wait_ge(dv_const, 2)
            rstd_1(0)
            masks(0, 0)
            residual(0, 0, 0)
            rstd_1(1)

            def rstd_2(i):
                after(gp, (mvar2, i + 1))
                gp.tensor_scalar(ve2[:], mv2[:, 1:2], EPS, 1.0, ALU.add, ALU.mult).then_inc(eps2, 1)
                gp.wait_ge(eps2, i + 1)
                gp.tensor_tensor(rs2[:], ve2[:], half_neg[:, 0:1], ALU.pow).then_inc(rstd2, 1)

            def copy_row(i, u4):
                after(gp, (xn2_done, i + 1))
                gp.tensor_copy(rows[:, u4, 1, 0:D], rows[:, u4, 0, 0:D]).then_inc(row_copy, 1)
                for k in range(TOP_K):
                    gp.tensor_copy(rows[:, u4, k, D:D + 1], token_id[:, bass.ds(i, 1)]).then_inc(row_copy, 1)

            def scatter(i, u4):
                after(gp, (slot_done, i + 1), (w_done, i + 1), (row_copy, 3 * (i + 1)))
                for k in range(TOP_K):
                    gp.indirect_dma_start(out=routed, out_offset=bass.IndirectOffsetOnAxis(ap=slot[:, u4, k:k + 1], axis=0),
                                          in_=rows[:, u4, k, :], in_offset=None).then_inc(scattered[u4], 16)

            def batch(b, u, n):
                for t in range(QT):
                    i = b * QT + t
                    u4 = u * QT + t
                    if known(i, 1):
                        rstd_2(i - 1)
                        copy_row(i - 1, (u4 - 1) % 4)
                    if t == 0 and below(b, B - 1):
                        masks(b + 1, 1 - u)
                        residual(b + 1, 1 - u, n + u)
                    if t == 1 and below(b, B - 2):
                        rstd_1(b + 2)
                    if known(i, 2):
                        scatter(i - 2, (u4 - 2) % 4)

            batches(gp, batch)
            rstd_2(NT - 1)
            copy_row(NT - 1, 3)
            scatter(NT - 2, 2)
            scatter(NT - 1, 3)

            def add_rows(t, u, q):
                after(gp, (ey_done, t + 1), (eid_done, t + 1), *([(added, 16 * t)] if known(t, 1) else []))
                gp.indirect_dma_start(out=out, out_offset=bass.IndirectOffsetOnAxis(ap=eid[:, u:u + 1], axis=0),
                                      in_=ey[:, u % 2, :], in_offset=None, compute_op=ALU.add).then_inc(added, 16)

            for done in x1_out:
                gp.wait_ge(done, 16 * B)
            gp.wait_ge(pad_out, 16 * (1 + E + SPARE))
            tiles(gp, add_rows)
            gp.wait_ge(added, 16 * MOE_T)

        @block.scalar
        def _(act):
            act.wait_ge(gates_in, 32)
            act.activation(tanhg[:], gates[:], ACT.Tanh).then_inc(tanh_done, 1)
            for n, name in enumerate(("wq", "wk", "wv", "wfc")):
                act.wait_ge(wT_ps, n + 1)
                act.copy(wT[name][:].rearrange("p c d -> p (c d)"), psS[:, n]).then_inc(wT_sb, 1)
            act.wait_ge(const_in, 16 * CONST_LOADS)

            def ctx_evac(b):
                act.wait_ge(ctxT_ps, b + 1)
                if known(b, 1):
                    act.wait_ge(v_ps, b)
                for c in range(DC):
                    src = psA[:, c * K2:(c + 1) * K2].rearrange("p (o k) -> p o k", o=1).to_broadcast([P, 3, K2])
                    act.copy(ctxT[:, c], src).then_inc(ctxT_sb, 1)

            def x_evac(b):
                act.wait_ge(xT_ps, b + 1)
                act.copy(xnT[:].rearrange("p c s -> p (c s)"), psA[:]).then_inc(xT_sb, 1)

            def q_evac(b, u):
                act.wait_ge(q_ps, b + 1)
                for a in range(2):
                    act.activation(qT[:, u, a], psA[:, a * S:(a + 1) * S], ACT.Identity, bias=bias[:, 0, a:a + 1]).then_inc(q_sb, 1)

            def t_evac(i, g):
                c0, c1 = T_GROUPS[g]
                act.wait_ge(t_ps, 3 * i + g + 1)
                if known(i, 1) and g == 0:
                    act.wait_ge(o_ps, i)
                act.copy(probT[:, c0:c1].rearrange("p c q -> p (c q)"), psT[:, 0:(c1 - c0) * P]).then_inc(t_sb, 1)

            def exp_scores(i, t):
                act.wait_ge(s_sub, i + 1)
                act.activation(prob[:, t, 0:HK], prob[:, t, 0:HK], ACT.Exp, scale=scale).then_inc(p_done, 1)

            def n2_evac(i):
                act.wait_ge(n2T_ps, i + 1)
                act.copy(xn2T[:].rearrange("p c q -> p (c q)"), psG[:, 0:D]).then_inc(n2T_sb, 1)

            def exp_gap(i):
                act.wait_ge(gap_done, i + 1)
                act.activation(egap[:], gap[:], ACT.Exp).then_inc(egap_done, 1)

            def o_evac(i):
                act.wait_ge(oT_ps, i + 1)
                for c in range(DC):
                    act.activation(onT[:, c], psB[:, c * P:(c + 1) * P], ACT.Identity, bias=bias[:, 2, c:c + 1]).then_inc(oT_sb, 1)

            ctx_evac(0)
            x_evac(0)
            q_evac(0, 0)
            for t in range(QT):
                exp_scores(t, t)

            def batch(b, u, n):
                for t in range(QT):
                    i = b * QT + t
                    t_evac(i, 0)
                    if t == 0 and below(b, B - 1):
                        ctx_evac(b + 1)
                    t_evac(i, 1)
                    if known(i, 1):
                        n2_evac(i - 1)
                    t_evac(i, 2)
                    if t == 0 and below(b, B - 1):
                        x_evac(b + 1)
                    if known(i, 1):
                        exp_gap(i - 1)
                    if t == 0 and below(b, B - 1):
                        q_evac(b + 1, 1 - u)
                    o_evac(i)
                    if below(b, B - 1):
                        exp_scores(i + 2, t)

            batches(act, batch)
            n2_evac(NT - 1)
            exp_gap(NT - 1)

            def e_evac(t, u):
                act.wait_ge(etT_ps, t + 1)
                act.copy(etT[:, u % 2].rearrange("p c q -> p (c q)"), psG[:, 0:D]).then_inc(etT_sb, 1)

            def silu(t, u):
                act.wait_ge(h0_ps, t + 1)
                if known(t, 2):
                    act.wait_ge(hg_done, t - 1)
                act.activation(hs[:, u % 2], psS[:, u % 2], ACT.Silu).then_inc(hs_done, 1)

            def y_evac(t, u):
                act.wait_ge(ey_ps, t + 1)
                if known(t, 2):
                    act.wait_ge(added, 16 * (t - 1))
                act.activation(ey[:, u % 2], psB[:, 0:D], ACT.Copy, scale=et[:, u, D + 1:D + 2]).then_inc(ey_done, 1)

            e_evac(0, 0)

            def tile(t, u, q):
                if below(t, MOE_T - 1):
                    e_evac(t + 1, u + 1)
                silu(t, u)
                if known(t, 1):
                    y_evac(t - 1, (u - 1) % 4)

            tiles(act, tile)
            y_evac(MOE_T - 1, 3)

        @block.vector
        def _(dve):
            dve.memset(pad_rows[:, 0:D], 0.0).then_inc(dv_const, 1)
            dve.memset(pad_rows[:, D + 1:D + 2], 0.0).then_inc(valid_done, 1)
            dve.memset(half_neg[:], -0.5).then_inc(valid_done, 1)
            dve.memset(ones[:], 1.0).then_inc(valid_done, 1)
            dve.memset(one_e[:], 1.0).then_inc(valid_done, 1)
            dve.wait_ge(iota_done, N_IOTA)
            dve.tensor_copy(pad_rows[:, D:D + 1], pad_i[:]).then_inc(valid_done, 1)
            dve.tensor_copy(token_id[:], token_i[:]).then_inc(valid_done, 1)
            dve.tensor_copy(expert_f[:], expert_i[:]).then_inc(valid_done, 1)
            dve.tensor_copy(tile_f[:], tile_i[:]).then_inc(valid_done, 1)
            dve.tensor_copy(head_f[:], head_i[:]).then_inc(valid_done, 1)
            dve.tensor_scalar(parity_i[:], parity_i[:], 4, 1, ALU.logical_shift_right, ALU.bitwise_and).then_inc(valid_done, 1)
            dve.wait_ge(valid_done, 10)
            dve.tensor_scalar(head_lt[:], head_f[:], K2 - 0.5, None, ALU.is_lt).then_inc(valid_done, 1)
            dve.tensor_copy(parity[:, 1:2], parity_i[:, 1:2]).then_inc(valid_done, 1)
            dve.tensor_scalar(parity[:, 0:1], parity_i[:, 0:1], -1.0, 1.0, ALU.mult, ALU.add).then_inc(valid_done, 1)
            dve.tensor_scalar(region0[:], expert_f[:, 0], float(REGION * P), None, ALU.mult).then_inc(valid_done, 1)
            dve.tensor_scalar(base[:], expert_f[:, 0], float(REGION * P), None, ALU.mult).then_inc(valid_done, 1)
            dve.wait_ge(valid_done, 15)
            dve.scalar_tensor_tensor(out=head_f[:], in0=head_f[:], scalar=-0.5, in1=head_lt[:], op0=ALU.is_gt, op1=ALU.mult).then_inc(valid_done, 1)
            dve.wait_ge(valid_done, 16)
            for c in range(CH):
                dve.tensor_copy(head_of[:, c], head_f[:, c, first_head[c]:first_head[c] + 3]).then_inc(valid_done, 1)
            dve.wait_ge(valid_done, 16 + CH)
            for u in range(2):
                dve.tensor_copy(vbd[:, u, :, :, HD], head_of[:]).then_inc(valid_done, 1)
            dve.wait_ge(mask_in, 16)
            dve.tensor_scalar(valid[:], mask_sb, 0, None, ALU.not_equal).then_inc(valid_done, 1)
            dve.tensor_scalar(masked[:], mask_sb, 0, MASKED / scale, ALU.is_equal, ALU.mult).then_inc(valid_done, 1)
            dve.wait_ge(const_in, 16 * CONST_LOADS)
            dve.wait_ge(tanh_done, 1)
            dve.tensor_scalar(bfc_rows[:], bfc_rows[:], tanhg[:, 0:1], None, ALU.mult).then_inc(valid_done, 1)
            dve.wait_ge(valid_done, 21 + CH)
            dve.memset(prob[:, :, HK:CH * P], 0.0).then_inc(valid_done, 1)
            dve.wait_ge(valid_done, 22 + CH)
            dve.engine_nop().then_inc(dv_const, 1)

            def stats_1(b, u, n):
                dve.wait_ge(x_in[u], 16 * (n + 1))
                if known(b, 1):
                    dve.wait_ge(rstd1, b)
                for t in range(QT):
                    dve.bn_stats(st1[:, t], xb[:, u, t]).then_inc(stat1, 1)
                after(dve, (stat1, QT * (b + 1)))
                for t in range(QT):
                    dve.bn_aggr(mv1[:, t], st1[:, t]).then_inc(mvar1, 1)

            def norm_1(b, u):
                dve.wait_ge(rstd1, b + 1)
                dve.wait_ge(mvar1, QT * (b + 1))
                if known(b, 1):
                    dve.wait_ge(xT_ps, b)
                for t in range(QT):
                    m = dve.tensor_scalar(xn[:, t], xb[:, u, t], mv1[:, t, 0:1], rs1[:, t:t + 1], ALU.subtract, ALU.mult)
                m.then_inc(xn_done, 1)

            def key_mask(b, u):
                if known(b, 2):
                    dve.wait_ge(k_sb, b - 1)
                for par in range(2):
                    dve.tensor_scalar(kmask[:, u, par], valid[:, bass.ds(b * K2, K2)], parity[:, par:par + 1], None, ALU.mult).then_inc(kmask_done, 1)

            def k_evac(b, u):
                dve.wait_ge(k_ps, b + 1)
                dve.wait_ge(kmask_done, 2 * (b + 1))
                for a in range(2):
                    src = psA[:, a * K2:(a + 1) * K2].rearrange("p (o k) -> p o k", o=1).to_broadcast([P, 2, K2])
                    m = dve.scalar_tensor_tensor(out=kbd[:, u, a], in0=src, scalar=bias[:, 1, a:a + 1], in1=kmask[:, u], op0=ALU.add, op1=ALU.mult)
                m.then_inc(k_sb, 1)

            def v_evac(b, u):
                dve.wait_ge(v_ps, b + 1)
                dve.tensor_tensor(vbd[:, u, :, :, 0:HD].rearrange("p c h d -> p (c h) d"),
                                  psA[:, 0:CH * 3 * HD].rearrange("p (n d) -> p n d", d=HD),
                                  head_of[:].rearrange("p c (h o) -> p (c h) o", o=1).to_broadcast([P, CH * 3, HD]), ALU.mult).then_inc(v_sb, 1)

            sv = psS[:, :, 0:2 * PAIR].rearrange("p r (h k) -> p r h k", k=K2)

            def softmax_shift(i, t):
                dve.wait_ge(s_ps, i + 1)
                m = mx[:, t].rearrange("p (r h) -> p r h", r=4)
                dve.tensor_reduce(m, sv, AX_X, ALU.max).then_inc(s_max, 1)
                dve.wait_ge(s_max, i + 1)
                dve.tensor_tensor(prob[:, t, 0:HK].rearrange("p (r h k) -> p r h k", r=4, k=K2), sv,
                                  m.rearrange("p r (h o) -> p r h o", o=1).to_broadcast([P, 4, 4, K2]), ALU.subtract).then_inc(s_sub, 1)

            def o_norm(i):
                dve.wait_ge(o_ps, i + 1)
                ov = psB[:, 0:H * VW].rearrange("p (h d) -> p h d", d=VW)
                dve.reciprocal(rden[:], ov[:, :, HD]).then_inc(o_rec, 1)
                dve.wait_ge(o_rec, i + 1)
                dve.tensor_tensor(on[:].rearrange("p (h d) -> p h d", d=HD), ov[:, :, 0:HD],
                                  rden[:].rearrange("p (h o) -> p h o", o=1).to_broadcast([P, H, HD]), ALU.mult).then_inc(o_sb, 1)

            def residual_1(i, u, t, b):
                dve.wait_ge(y_ps, i + 1)
                dve.wait_ge(xg_done, QT * (b + 1))
                if known(b, 1):
                    dve.wait_ge(x1_out[t], 16 * b)
                dve.scalar_tensor_tensor(out=x1[:, t], in0=psB[:, 0:D], scalar=tanhg[:, 0:1], in1=xg[:, u, t], op0=ALU.mult, op1=ALU.add).then_inc(x1_done, 1)
                dve.wait_ge(x1_done, i + 1)
                dve.bn_stats(st2[:], x1[:, t]).then_inc(stat2, 1)
                after(dve, (stat2, i + 1))
                dve.bn_aggr(mv2[:], st2[:]).then_inc(mvar2, 1)

            def norm_2(i, t, u4, n):
                dve.wait_ge(rstd2, i + 1)
                dve.wait_ge(mvar2, i + 1)
                if known(n, 1):
                    dve.wait_ge(scattered[u4], 32 * n)
                dve.tensor_scalar(rows[:, u4, 0, 0:D], x1[:, t], mv2[:, 0:1], rs2[:, 0:1], ALU.subtract, ALU.mult).then_inc(xn2_done, 1)

            def choose(i):
                dve.wait_ge(g_ps, i + 1)
                dve.tensor_copy(logit[:], psG[:, D:D + E]).then_inc(l_cp, 1)
                after(dve, (l_cp, i + 1))
                dve.max(top[:], logit[:]).then_inc(l_max, 1)
                after(dve, (l_max, i + 1))
                dve.max_index(topi[:], top[:], logit[:]).then_inc(l_idx, 1)
                if known(i, 1):
                    dve.wait_ge(egap_done, i)
                dve.tensor_tensor(gap[:], top[:, 1:2], top[:, 0:1], ALU.subtract).then_inc(gap_done, 1)
                dve.wait_ge(l_idx, i + 1)
                dve.tensor_copy(topf[:], topi[:, 0:TOP_K]).then_inc(l_idf, 1)
                dve.wait_ge(l_idf, i + 1)
                dve.tensor_tensor(chosen[:], expert_f[:], topf[:].rearrange("p (k o) -> p k o", o=1).to_broadcast([P, TOP_K, E]), ALU.is_equal).then_inc(l_oh, 1)
                dve.wait_ge(l_oh, i + 1)
                dve.tensor_tensor(chosen_any[:], chosen[:, 0], chosen[:, 1], ALU.add).then_inc(l_any, 1)

            def place(i, u4):
                dve.wait_ge(r_ps, i + 1)
                dve.tensor_tensor(pos[:], psG[:, D + E:D + 2 * E], base[:], ALU.add).then_inc(pos_done, 1)
                dve.wait_ge(egap_done, i + 1)
                dve.tensor_scalar(wsum[:], egap[:], 1.0, None, ALU.add).then_inc(w_sum, 1)
                dve.wait_ge(pos_done, i + 1)
                dve.tensor_tensor(base[:], psG[:, D + 2 * E:D + 3 * E], base[:], ALU.add).then_inc(base_done, 1)
                dve.tensor_tensor(picked[:], chosen[:], pos[:].rearrange("p (o e) -> p o e", o=1).to_broadcast([P, TOP_K, E]), ALU.mult).then_inc(pick_done, 1)
                dve.wait_ge(w_sum, i + 1)
                dve.reciprocal(wrec[:], wsum[:]).then_inc(w_rec, 1)
                dve.wait_ge(pick_done, i + 1)
                dve.tensor_reduce(slotf[:], picked[:], AX_X, ALU.add).then_inc(slotf_done, 1)
                dve.wait_ge(w_rec, i + 1)
                dve.tensor_tensor(rows[:, u4, 0, D + 1:D + 2], wrec[:], tanhg[:, 1:2], ALU.mult).then_inc(w_one, 1)
                dve.wait_ge(slotf_done, i + 1)
                dve.tensor_copy(slot[:, u4], slotf[:]).then_inc(slot_done, 1)
                dve.wait_ge(w_one, i + 1)
                dve.tensor_tensor(rows[:, u4, 1, D + 1:D + 2], rows[:, u4, 0, D + 1:D + 2], egap[:], ALU.mult).then_inc(w_done, 1)
                dve.wait_ge(base_done, i + 1)

            stats_1(0, 0, 0)
            norm_1(0, 0)
            key_mask(0, 0)
            k_evac(0, 0)
            v_evac(0, 0)
            stats_1(1, 1, 0)
            norm_1(1, 1)
            for t in range(QT):
                softmax_shift(t, t)

            def batch(b, u, n):
                for t in range(QT):
                    i = b * QT + t
                    u4 = u * QT + t
                    if known(i, 1):
                        residual_1(i - 1, u if t else 1 - u, 1 - t, b if t else b - 1)
                    if t == 0 and below(b, B - 1):
                        key_mask(b + 1, 1 - u)
                        k_evac(b + 1, 1 - u)
                    if t == 1 and below(b, B - 1):
                        v_evac(b + 1, 1 - u)
                    if known(i, 1):
                        norm_2(i - 1, 1 - t, (u4 - 1) % 4, n if u4 else n - 1)
                    if t == 1 and below(b, B - 2):
                        stats_1(b + 2, u, n + 1)
                    if known(i, 1):
                        choose(i - 1)
                    o_norm(i)
                    if below(b, B - 1):
                        softmax_shift(i + 2, t)
                    if known(i, 1):
                        place(i - 1, (u4 - 1) % 4)
                    if t == 1 and below(b, B - 2):
                        norm_1(b + 2, u)

            batches(dve, batch)
            residual_1(NT - 1, 1, 1, B - 1)
            norm_2(NT - 1, 1, 3, LOOPS - 1)
            choose(NT - 1)
            place(NT - 1, 3)

            steps = [0]

            def step(m):
                m.then_inc(tab, 1)
                steps[0] += 1
                dve.wait_ge(tab, steps[0])

            step(dve.tensor_copy(base_i[:], base[:]))
            step(dve.tensor_tensor(cnt_f[:], base[:], region0[:], ALU.subtract))
            step(dve.tensor_scalar(cnt_f[:], cnt_f[:], float(P - 1), None, ALU.add))
            step(dve.tensor_copy(cnt_i[:], cnt_f[:]))
            step(dve.tensor_scalar(nt_i[:], cnt_i[:], P.bit_length() - 1, None, ALU.logical_shift_right))
            step(dve.tensor_copy(nt_f[:], nt_i[:]))
            step(dve.tensor_tensor_scan(tend[:], one_e[:], nt_f[:], 0.0, ALU.mult, ALU.add))
            step(dve.tensor_scalar(skip[:], nt_f[:], -1.0, float(REGION), ALU.mult, ALU.add))
            step(dve.tensor_tensor(past[:], tile_f[:].rearrange("p (t o) -> p t o", o=1).to_broadcast([P, MOE_T, E]),
                                   tend[:].rearrange("p (o e) -> p o e", o=1).to_broadcast([P, MOE_T, E]), ALU.is_ge))
            step(dve.tensor_reduce(texp[:], past[:], AX_X, ALU.add))
            step(dve.tensor_scalar(texp2[:], texp[:], float(E - 1), None, ALU.min))
            step(dve.tensor_copy(texp_i[:], texp2[:]))
            step(dve.tensor_tensor(past[:], past[:], skip[:].rearrange("p (o e) -> p o e", o=1).to_broadcast([P, MOE_T, E]), ALU.mult))
            step(dve.tensor_reduce(tblk[:], past[:], AX_X, ALU.add))
            step(dve.tensor_tensor(tblk[:], tblk[:], tile_f[:], ALU.add))
            step(dve.tensor_copy(tblk_i[:], tblk[:]))
            dve.engine_nop().then_inc(tab_done, 1)

            def glu(t, u):
                dve.wait_ge(h1_ps, t + 1)
                dve.wait_ge(hs_done, t + 1)
                if known(t, 2):
                    dve.wait_ge(hgT_ps, t - 1)
                dve.tensor_tensor(hg[:, u % 2], psS[:, 2 + u % 2], hs[:, u % 2], ALU.mult).then_inc(hg_done, 1)

            def g_evac(t, u):
                dve.wait_ge(hgT_ps, t + 1)
                if known(t, 2):
                    dve.wait_ge(ey_ps, t - 1)
                dve.tensor_copy(hgT[:, u % 2].rearrange("p c q -> p (c q)"), psT[:]).then_inc(hgT_sb, 1)

            def tile(t, u, q):
                dve.wait_ge(et_in[u], 16 * (q + 1))
                if known(t, 4):
                    dve.wait_ge(added, 16 * (t - 3))
                dve.tensor_copy(eid[:, u:u + 1], et[:, u, D:D + 1]).then_inc(eid_done, 1)
                if known(t, 1):
                    g_evac(t - 1, (u - 1) % 4)
                glu(t, u)

            tiles(dve, tile)
            g_evac(MOE_T - 1, 3)

        @block.tensor
        def _(pe):
            pe.wait_ge(ident_done, 2)
            pe.wait_ge(raw_in, 16 * 18)
            for n in range(4):
                for c in range(DC):
                    for o in range(DC):
                        m = pe.transpose(psS[:, n, (c * DC + o) * P:(c * DC + o + 1) * P], raw[:, n, o, c * P:(c + 1) * P], ident[:])
                m.then_inc(wT_ps, 1)

            def ctx_T(b, u, n):
                pe.wait_ge(ctx_in_s[u], 16 * (n + 1))
                if known(b, 1):
                    pe.wait_ge(v_sb, b)
                for c in range(DC):
                    m = pe.transpose(psA[:, c * K2:(c + 1) * K2], cb[:, u, c * P:(c + 1) * P], ident[0:K2, 0:K2])
                m.then_inc(ctxT_ps, 1)

            def keys(b):
                pe.wait_ge(ctxT_sb, DC * (b + 1))
                for a in range(2):
                    for c in range(DC):
                        m = pe.matmul(psA[:, a * K2:(a + 1) * K2], wT["wk"][:, c, a * P:(a + 1) * P], ctxT[:, c, 0], start=(c == 0), stop=(c == DC - 1))
                m.then_inc(k_ps, 1)

            def x_T(b):
                pe.wait_ge(xn_done, b + 1)
                pe.wait_ge(k_sb, b + 1)
                for c in range(DC):
                    for t in range(QT):
                        m = pe.transpose(psA[:, c * S + t * P:c * S + (t + 1) * P], xn[:, t, c * P:(c + 1) * P], ident[:])
                m.then_inc(xT_ps, 1)

            def queries(b):
                pe.wait_ge(xT_sb, b + 1)
                for a in range(2):
                    for c in range(DC):
                        m = pe.matmul(psA[:, a * S:(a + 1) * S], wT["wq"][:, c, a * P:(a + 1) * P], xnT[:, c], start=(c == 0), stop=(c == DC - 1))
                m.then_inc(q_ps, 1)

            def values(b, part):
                if part == 0:
                    pe.wait_ge(q_sb, 2 * (b + 1))
                half = CH // 2
                for j in range(half * part, half * part + half if part == 0 else CH):
                    s = P * j % K2
                    h = first_head[j]
                    for c in range(DC):
                        lhsT = ctxT[:, c].rearrange("p o k -> p (o k)")[:, s:s + P]
                        m = pe.matmul(psA[:, j * 3 * HD:(j + 1) * 3 * HD], lhsT, wT["wv"][:, c, h * HD:(h + 3) * HD], start=(c == 0), stop=(c == DC - 1))
                if part == 1:
                    m.then_inc(v_ps, 1)

            def scores(i, u, t, b):
                pe.wait_ge(q_sb, 2 * (b + 1))
                pe.wait_ge(k_sb, b + 1)
                pe.wait_ge(mrow_done, b + 1)
                if known(i, 1):
                    pe.wait_ge(s_sub, i)
                for r in range(4):
                    q = slice(32 * r, 32 * r + 32)
                    pe.matmul(psS[:, r, 0:2 * PAIR], ones[32 * r:32 * r + 1, :], mrow[32 * r:32 * r + 1, u].rearrange("p h k -> p (h k)"),
                              start=True, stop=False, skip_group_check=True)
                    for a in range(2):
                        m = pe.matmul(psS[:, r, a * PAIR:(a + 1) * PAIR], qT[q, u, a, t * P:(t + 1) * P],
                                      kbd[q, u, a].rearrange("p h k -> p (h k)"), start=False, stop=True, skip_group_check=True)
                m.then_inc(s_ps, 1)

            def prob_T(i, t, g):
                c0, c1 = T_GROUPS[g]
                if g == 0:
                    pe.wait_ge(p_done, i + 1)
                if known(3 * i + g, 1):
                    pe.wait_ge(t_sb, 3 * i + g)
                for c in range(c0, c1):
                    m = pe.transpose(psT[:, (c - c0) * P:(c - c0 + 1) * P], prob[:, t, c * P:(c + 1) * P], ident[:])
                m.then_inc(t_ps, 1)

            def attend(i, u, b):
                pe.wait_ge(t_sb, 3 * (i + 1))
                pe.wait_ge(v_sb, b + 1)
                if known(i, 1):
                    pe.wait_ge(x1_done, i)
                for c in range(CH):
                    h = first_head[c]
                    m = pe.matmul(psB[:, h * VW:(h + 3) * VW], probT[:, c], vbd[:, u, c].rearrange("p h d -> p (h d)"),
                                  start=(c == 0), stop=(c == CH - 1), skip_group_check=True)
                m.then_inc(o_ps, 1)

            def o_T(i):
                pe.wait_ge(o_sb, i + 1)
                for c in range(DC):
                    m = pe.transpose(psB[:, c * P:(c + 1) * P], on[:, c * P:(c + 1) * P], ident[:])
                m.then_inc(oT_ps, 1)

            def project(i):
                pe.wait_ge(oT_sb, DC * (i + 1))
                for c in range(DC):
                    m = pe.matmul(psB[:, 0:D], onT[:, c], wT["wfc"][:, c], start=(c == 0), stop=(c == DC - 1))
                m.then_inc(y_ps, 1)

            def n2_T(i, u4):
                pe.wait_ge(xn2_done, i + 1)
                if known(i, 1):
                    pe.wait_ge(base_done, i)
                for c in range(DC):
                    m = pe.transpose(psG[:, c * P:(c + 1) * P], rows[:, u4, 0, c * P:(c + 1) * P], ident[:])
                m.then_inc(n2T_ps, 1)

            def gate(i):
                pe.wait_ge(n2T_sb, i + 1)
                for c in range(DC):
                    m = pe.matmul(psG[:, D:D + E], xn2T[:, c], gate_sb[:, c], start=(c == 0), stop=(c == DC - 1))
                m.then_inc(g_ps, 1)

            def rank(i):
                pe.wait_ge(l_any, i + 1)
                pe.matmul(psG[:, D + E:D + 2 * E], upper[:], chosen_any[:], start=True, stop=True)
                pe.matmul(psG[:, D + 2 * E:D + 3 * E], ones[:], chosen_any[:], start=True, stop=True).then_inc(r_ps, 1)

            pe.wait_ge(wT_sb, 4)
            pe.wait_ge(dv_const, 2)
            pe.wait_ge(gate_in, 16)
            ctx_T(0, 0, 0)
            keys(0)
            x_T(0)
            queries(0)
            values(0, 0)
            values(0, 1)
            scores(0, 0, 0, 0)
            scores(1, 0, 1, 0)

            def batch(b, u, n):
                more = below(b, B - 1)
                for t in range(QT):
                    i = b * QT + t
                    u4 = u * QT + t
                    prob_T(i, t, 0)
                    if more:
                        ctx_T(b + 1, 1 - u, n + u) if t == 0 else values(b + 1, 0)
                    prob_T(i, t, 1)
                    if more:
                        keys(b + 1) if t == 0 else values(b + 1, 1)
                    if known(i, 1):
                        n2_T(i - 1, (u4 - 1) % 4)
                    prob_T(i, t, 2)
                    if more and t == 0:
                        x_T(b + 1)
                    if known(i, 1):
                        gate(i - 1)
                    attend(i, u, b)
                    if more and t == 0:
                        queries(b + 1)
                    if more:
                        scores(i + 2, 1 - u, t, b + 1)
                    if known(i, 1):
                        rank(i - 1)
                    o_T(i)
                    project(i)

            batches(pe, batch)
            n2_T(NT - 1, 3)
            gate(NT - 1)
            rank(NT - 1)

            pe.wait_ge(moe_in, 16 * 3 * E)
            pe.wait_ge(tab_done, 1)

            def e_T(t, u, q):
                pe.wait_ge(et_in[u], 16 * (q + 1))
                if known(t, 1):
                    pe.wait_ge(etT_sb, t)
                for c in range(DC):
                    m = pe.transpose(psG[:, c * P:(c + 1) * P], et[:, u, c * P:(c + 1) * P], ident[:])
                m.then_inc(etT_ps, 1)

            def up(t, u, e, w, bank, done):
                for c in range(DC):
                    m = pe.matmul(psS[:, bank], etT[:, u % 2, c], w[:].rearrange("p e c f -> p (e c) f")[:, bass.ds(e * DC + c, 1), :].rearrange("p o f -> p (o f)"),
                                  start=(c == 0), stop=(c == DC - 1))
                m.then_inc(done, 1)

            def g_T(t, u):
                pe.wait_ge(hg_done, t + 1)
                if known(t, 1):
                    pe.wait_ge(hgT_sb, t)
                for c in range(FC):
                    m = pe.transpose(psT[:, c * P:(c + 1) * P], hg[:, u % 2, c * P:(c + 1) * P], ident[:])
                m.then_inc(hgT_ps, 1)

            def down(t, u, e):
                pe.wait_ge(hgT_sb, t + 1)
                if known(t, 1):
                    pe.wait_ge(ey_done, t)
                for c in range(FC):
                    m = pe.matmul(psB[:, 0:D], hgT[:, u % 2, c], wo_sb[:].rearrange("p e c d -> p (e c) d")[:, bass.ds(e * FC + c, 1), :].rearrange("p o d -> p (o d)"),
                                  start=(c == 0), stop=(c == FC - 1))
                m.then_inc(ey_ps, 1)

            def expert_of(t):
                return pe.value_load(texp_i[0:1, bass.ds(t, 1)], min_val=0, max_val=E - 1)

            e_T(0, 0, 0)

            def tile(t, u, q):
                e = expert_of(t)
                pe.wait_ge(etT_sb, t + 1)
                if known(t, 2):
                    pe.wait_ge(hg_done, t - 1)
                up(t, u, e, w0_sb, u % 2, h0_ps)
                if known(t, 1):
                    g_T(t - 1, (u - 1) % 4)
                if below(t, MOE_T - 1):
                    e_T(t + 1, (u + 1) % 4, q + (u == 3))
                up(t, u, e, w1_sb, 2 + u % 2, h1_ps)
                if known(t, 1):
                    down(t - 1, (u - 1) % 4, expert_of(t - 1))

            tiles(pe, tile)
            g_T(MOE_T - 1, 3)
            down(MOE_T - 1, 3, expert_of(MOE_T - 1))


_INS = ["x", "ctx_1024", "mask_BxS2_ik0", "g_xattn", "g_ffn",
        "L0_xattn_Wq", "L0_xattn_bq", "L0_xattn_Wk", "L0_xattn_bk", "L0_xattn_Wv", "L0_xattn_bv",
        "L0_xattn_Wfc", "L0_xattn_bfc", "L0_ffn_gate_kernel", "L0_ffn_w0_kernel", "L0_ffn_w1_kernel",
        "L0_ffn_wo_kernel"]


def kernel(**inputs):
    import numpy as _np
    import concourse.bacc as _bacc
    from concourse import mybir as _mybir
    from concourse.bass_utils import run_bass_kernel_spmd as _run

    nc = _bacc.Bacc("TRN2", target_bir_lowering=False, num_devices=1)
    arrays, args = {}, []
    for name in _INS:
        a = _np.ascontiguousarray(inputs[name])
        arrays[f"in_{name}_dram"] = a
        args.append(nc.dram_tensor(f"in_{name}_dram", a.shape, _mybir.dt.from_np(a.dtype), kind="ExternalInput").ap())
    B, S, D = inputs["x"].shape
    args.append(nc.dram_tensor("out_0_dram", (B * S + P, D), F32, kind="ExternalOutput").ap())
    flamingo_gated_layer(nc, *args)
    r = _run(nc, [arrays], core_ids=[0])
    return r.results[0]["out_0_dram"][:B * S].reshape(B, S, D)
```

```python
from contextlib import ExitStack

import concourse.bass as bass
from concourse import mybir

F32 = mybir.dt.float32
BF16 = mybir.dt.bfloat16
I32 = mybir.dt.int32
U32 = mybir.dt.uint32
ALU = mybir.AluOpType
ACT = mybir.ActivationFunctionType
AX_X = mybir.AxisListType.X

P = 128
EPS = 1e-5
MASKED = -1e10
TOP_K = 2
ROW = 2


def flamingo_gated_layer(nc, x, ctx_in, mask, g_xattn, g_ffn, Wq, bq, Wk, bk, Wv, bv, Wfc, bfc,
                         gate_kernel, w0, w1, wo, out):
    B, S, D = x.shape
    K2 = ctx_in.shape[1]
    HD = 16
    H = D // HD
    QT = S // P
    NT = B * QT
    DC = D // P
    E, _, F = w0.shape
    FC = F // P
    scale = float(HD) ** -0.5
    assert QT == 2 and DC == 2 and B % 4 == 0

    HB = 512 // K2
    HC = P // HD
    S_BANKS = [(n, h, min(HB, H - h)) for n, h in enumerate(range(0, H, HB))]
    S_PIECES = [(n, c, max(h, c * HC), min(h + k, (c + 1) * HC)) for n, h, k in S_BANKS for c in range(DC)
                if max(h, c * HC) < min(h + k, (c + 1) * HC)]
    S_FULL = H // HB
    assert len(S_BANKS) == 3 and S_FULL == 2
    HK = H * K2
    CH = -(-HK // P)
    first_head = [min(P * c // K2, H - 3) for c in range(CH)]
    VW = HD + 1
    T_GROUPS = [(0, 4), (4, 8), (8, CH)]

    REGION = NT + 1
    MOE_T = NT * TOP_K + E
    SPARE = MOE_T - NT * TOP_K + 1
    RW = D + ROW
    routed = nc.dram_tensor("routed_rows", [(E * REGION + SPARE) * P, RW], F32, kind="Internal").ap()

    x_t = x.rearrange("b (t p) d -> b p t d", p=P)
    gx = g_xattn.rearrange("(o a) -> o a", o=1)
    gf = g_ffn.rearrange("(o a) -> o a", o=1)

    with ExitStack() as ctx:
        def sb(name, shape, dt=F32):
            return ctx.enter_context(nc.sbuf_tensor(name, shape, dt))

        def ps(name, shape, dt=F32):
            return ctx.enter_context(nc.psum_tensor(name, shape, dt))

        def sem(name):
            return ctx.enter_context(nc.semaphore(name))

        w0_sb = sb("w0_sb", [P, E, DC, F])
        w1_sb = sb("w1_sb", [P, E, DC, F])
        wo_sb = sb("wo_sb", [P, E, FC, D])
        wT = {n: sb(f"{n}T", [P, DC, D]) for n in ("wq", "wk", "wv", "wfc")}
        gate_sb = sb("gate_sb", [P, DC, E])
        bias = sb("bias", [P, 3, DC])
        bfc_rows = sb("bfc_rows", [P, D])
        gates = sb("gates", [P, 2])
        tanhg = sb("tanhg", [P, 2])
        ident = sb("ident", [P, P])
        upper = sb("upper", [P, P], BF16)
        ones = sb("ones", [P, P], BF16)
        valid = sb("valid", [P, B * K2], BF16)
        masked = sb("masked", [P, B * K2], BF16)
        own_i = sb("own_i", [P, HC], I32)
        own_f = sb("own_f", [P, HC])
        own_lt = sb("own_lt", [P, HC])
        own = sb("own", [P, HC])
        head_i = sb("head_i", [P, CH, H], I32)
        head_f = sb("head_f", [P, CH, H])
        head_lt = sb("head_lt", [P, CH, H])
        head_of = sb("head_of", [P, CH, 3])
        token_id = sb("token_id", [P, NT])
        token_i = sb("token_i", [P, NT], I32)
        expert_i = sb("expert_i", [P, 2, E], I32)
        expert_f = sb("expert_f", [P, 2, E])
        half_neg = sb("half_neg", [P, 2])
        region0 = sb("region0", [P, E])
        pad_rows = sb("pad_rows", [P, RW])
        pad_i = sb("pad_i", [P, 1], I32)

        xb = sb("xb", [P, 2, QT, D])
        xg = sb("xg", [P, 2, QT, D])
        cb = sb("cb", [K2, 2, D])
        xn = sb("xn", [P, QT, D])
        xnT = sb("xnT", [P, DC, S])
        ctxT = sb("ctxT", [P, DC, 3, K2])
        qT = sb("qT", [P, 2, 2, S])
        kT = sb("kT", [P, DC, K2])
        kbd = sb("kbd", [P, 2, DC, HC, K2])
        mrow = sb("mrow", [P, 2, K2], BF16)
        vbd = sb("vbd", [P, 2, CH, 3, VW])
        prob = sb("prob", [P, 2, CH * P])
        probT = sb("probT", [P, CH, P])
        mx = sb("mx", [P, 2, H])
        rden = sb("rden", [P, H])
        on = sb("on", [P, D])
        onT = sb("onT", [P, DC, P])
        x1 = sb("x1", [P, 2, D])
        st1 = sb("st1", [P, QT, 6])
        mv1 = sb("mv1", [P, QT, 2])
        ve1 = sb("ve1", [P, QT])
        rs1 = sb("rs1", [P, QT])
        st2 = sb("st2", [P, 6])
        mv2 = sb("mv2", [P, 2])
        ve2 = sb("ve2", [P, 1])
        rs2 = sb("rs2", [P, 1])
        rows = sb("rows", [P, 4, TOP_K, RW])
        xn2T = sb("xn2T", [P, DC, P])
        logit = sb("logit", [P, E])
        top = sb("top", [P, 8])
        topi = sb("topi", [P, 8], U32)
        topf = sb("topf", [P, TOP_K])
        chosen = sb("chosen", [P, TOP_K, E])
        chosen_any = sb("chosen_any", [P, E], BF16)
        gap = sb("gap", [P, 1])
        egap = sb("egap", [P, 1])
        wsum = sb("wsum", [P, 1])
        wrec = sb("wrec", [P, 1])
        pos = sb("pos", [P, E])
        base = sb("base", [P, E])
        picked = sb("picked", [P, TOP_K, E])
        slotf = sb("slotf", [P, TOP_K])
        slot = sb("slot", [P, 4, TOP_K], I32)
        base_i = sb("base_i", [P, E], I32)
        cnt_f = sb("cnt_f", [P, E])
        cnt_i = sb("cnt_i", [P, E], I32)
        nt_i = sb("nt_i", [P, E], I32)
        nt_f = sb("nt_f", [P, E])
        one_e = sb("one_e", [P, E])
        tend = sb("tend", [P, E])
        skip = sb("skip", [P, E])
        tile_i = sb("tile_i", [P, MOE_T], I32)
        tile_f = sb("tile_f", [P, MOE_T])
        past = sb("past", [P, MOE_T, E])
        texp = sb("texp", [P, MOE_T])
        texp2 = sb("texp2", [P, MOE_T])
        tblk = sb("tblk", [P, MOE_T])
        texp_i = sb("texp_i", [P, MOE_T], I32)
        tblk_i = sb("tblk_i", [P, MOE_T], I32)
        mask_sb = prob[:].rearrange("p t n -> p (t n)").bitcast(I32)[:, 0:B * K2]

        et = sb("et", [P, 4, RW])
        hbuf = sb("hbuf", [P, 4, F])
        hs, hg = hbuf[:, 0:2], hbuf[:, 2:4]
        raw = hbuf[:].rearrange("p n (c d) -> p n c d", c=DC)
        kbd_flat = kbd[:].rearrange("p u c h k -> p (u c h k)")
        hgT = kbd_flat[:, 0:2 * F].rearrange("p (u c q) -> p u c q", u=2, c=FC)
        etT = kbd_flat[:, 2 * F:2 * F + 2 * D].rearrange("p (u c q) -> p u c q", u=2, c=DC)
        ey = sb("ey", [P, 2, D])
        eid = sb("eid", [P, 4], I32)

        banks4 = ps("banks4", [P, 4, 512])
        psS, psK = banks4[:, 0:3], banks4[:, 3]
        psT = ps("psT", [P, 512])
        psG = ps("psG", [P, 512])
        psA = ps("psA", [P, 512])
        psB = ps("psB", [P, 512])

        raw_in, const_in, mask_in, gates_in = sem("raw_in"), sem("const_in"), sem("mask_in"), sem("gates_in")
        gate_in, moe_in, x_in, ctx_in_s = sem("gate_in"), sem("moe_in"), [sem("x_in0"), sem("x_in1")], [sem("ctx_in0"), sem("ctx_in1")]
        x1_out, pad_out, scattered = [sem("x1_out0"), sem("x1_out1")], sem("pad_out"), [sem(f"scattered{j}") for j in range(4)]
        iota_done, ident_done, dv_const, sel_done = sem("iota_done"), sem("ident_done"), sem("dv_const"), sem("sel_done")
        wT_ps, wT_sb, tanh_done, valid_done = sem("wT_ps"), sem("wT_sb"), sem("tanh_done"), sem("valid_done")
        stat1, mvar1, eps1, rstd1, xn_done = sem("stat1"), sem("mvar1"), sem("eps1"), sem("rstd1"), sem("xn_done")
        xg_done, kbd_done, mrow_done = sem("xg_done"), sem("kbd_done"), sem("mrow_done")
        ctxT_ps, ctxT_sb, xT_ps, xT_sb = sem("ctxT_ps"), sem("ctxT_sb"), sem("xT_ps"), sem("xT_sb")
        k_ps, k_sb, q_ps, q_sb, v_ps, v_sb = (sem(n) for n in ("k_ps", "k_sb", "q_ps", "q_sb", "v_ps", "v_sb"))
        s_ps, s_max, s_sub, p_done = sem("s_ps"), sem("s_max"), sem("s_sub"), sem("p_done")
        t_ps, t_sb, o_ps, o_rec, o_sb = sem("t_ps"), sem("t_sb"), sem("o_ps"), sem("o_rec"), sem("o_sb")
        oT_ps, oT_sb, y_ps, x1_done = sem("oT_ps"), sem("oT_sb"), sem("y_ps"), sem("x1_done")
        stat2, mvar2, eps2, rstd2, xn2_done = sem("stat2"), sem("mvar2"), sem("eps2"), sem("rstd2"), sem("xn2_done")
        n2T_ps, n2T_sb, g_ps, r_ps = sem("n2T_ps"), sem("n2T_sb"), sem("g_ps"), sem("r_ps")
        l_cp, l_max, l_idx, l_idf, l_oh, l_any, gap_done = (
            sem(n) for n in ("l_cp", "l_max", "l_idx", "l_idf", "l_oh", "l_any", "gap_done"))
        egap_done, w_sum, w_rec, w_one, w_done = (sem(n) for n in ("egap_done", "w_sum", "w_rec", "w_one", "w_done"))
        pos_done, base_done, pick_done, slotf_done, slot_done = (
            sem(n) for n in ("pos_done", "base_done", "pick_done", "slotf_done", "slot_done"))
        row_copy, row_id = sem("row_copy"), sem("row_id")
        passed = {e.engine: sem(f"passed{n}") for n, e in enumerate((nc.sync, nc.gpsimd, nc.vector))}
        tab, tab_done = sem("tab"), sem("tab_done")
        et_in, etT_ps, etT_sb, h0_ps, h1_ps = [sem(f"et_in{j}") for j in range(4)], sem("etT_ps"), sem("etT_sb"), sem("h0_ps"), sem("h1_ps")
        hs_done, hg_done, hgT_ps, hgT_sb, ey_ps, ey_done, eid_done, added = (
            sem(n) for n in ("hs_done", "hg_done", "hgT_ps", "hgT_sb", "ey_ps", "ey_done", "eid_done", "added"))

        CONST_LOADS = 1 + 3 * 2
        N_IOTA, N_SEL = 8, 3
        UNR = 2
        LOOPS = B // UNR
        PEELED = 2

        def batches(eng, body):
            for b in range(PEELED * UNR):
                body(b, b % UNR, b // UNR)
            with eng.Fori(PEELED, LOOPS - 1) as it:
                for u in range(UNR):
                    body(it * UNR + u, u, it)
            for u in range(UNR):
                body(B - UNR + u, u, LOOPS - 1)

        def tiles(eng, body, n=MOE_T, unroll=4):
            for u in range(unroll):
                body(u, u, 0)
            with eng.Fori(1, n // unroll - 1) as it:
                for u in range(unroll):
                    body(it * unroll + u, u, it)
            for u in range(unroll):
                body(n - unroll + u, u, n // unroll - 1)

        def known(v, least):
            return not isinstance(v, int) or v >= least

        def below(v, end):
            return not isinstance(v, int) or v < end

        def after(eng, *waits):
            for done, v in waits:
                eng.wait_ge(done, v)
            if waits:
                eng.sem_inc(passed[eng.engine], 1)

        block = ctx.enter_context(nc.Block())

        @block.sync
        def _(sp):
            def load_batch(b, u):
                sp.dma_start(xb[:, u], x_t[b] if isinstance(b, int) else x_t[bass.ds(b, 1)].rearrange("o p t d -> p (o t) d")).then_inc(x_in[u], 16)
                sp.dma_start(cb[:, u], ctx_in[b] if isinstance(b, int) else ctx_in[bass.ds(b, 1)].rearrange("o k d -> k (o d)")).then_inc(ctx_in_s[u], 16)

            sp.dma_start(xb[:, 0], x_t[0]).then_inc(x_in[0], 16)
            sp.dma_start(cb[:, 0], ctx_in[0]).then_inc(ctx_in_s[0], 16)
            for n, w in enumerate((Wk, Wq, Wv, Wfc)):
                sp.dma_start(raw[:, n], w.rearrange("(c p) d -> p c d", p=P)).then_inc(raw_in, 16)
            load_batch(1, 1)
            sp.dma_start(mask_sb, mask.rearrange("b k -> (b k)").rearrange("(o n) -> o n", o=1).to_broadcast([P, B * K2])).then_inc(mask_in, 16)
            sp.dma_start(gate_sb[:], gate_kernel.rearrange("(c p) e -> p c e", p=P)).then_inc(gate_in, 16)
            sp.wait_ge(dv_const, 1)
            sp.dma_start(out[NT * P:NT * P + P, :], pad_rows[:, 0:D]).then_inc(pad_out, 16)
            for e in range(E):
                sp.dma_start(w0_sb[:, e], w0[e].rearrange("(c p) f -> p c f", p=P)).then_inc(moe_in, 16)
                sp.dma_start(w1_sb[:, e], w1[e].rearrange("(c p) f -> p c f", p=P)).then_inc(moe_in, 16)
                sp.dma_start(wo_sb[:, e], wo[e].rearrange("(c p) d -> p c d", p=P)).then_inc(moe_in, 16)

            def store_x1(i, slot_):
                sp.wait_ge(x1_done, i + 1)
                dst = out[i * P:(i + 1) * P, :] if isinstance(i, int) else out[bass.ds(i * P, P), :]
                sp.dma_start(dst, x1[:, slot_]).then_inc(x1_out[slot_], 16)

            def batch(b, u, n):
                if known(b, 1):
                    store_x1(b * QT - 1, 1)
                if below(b, B - 2):
                    after(sp, (xn_done, b + 1))
                    after(sp, (xg_done, QT * (b + 1)))
                    after(sp, (ctxT_ps, b + 1))
                    load_batch(b + 2, u)
                store_x1(b * QT, 0)

            batches(sp, batch)
            store_x1(NT - 1, 1)

            sp.wait_ge(tab_done, 1)
            for done in scattered:
                sp.wait_ge(done, 32 * NT // 4)
            for e in range(E):
                r = sp.value_load(base_i[0:1, e:e + 1], min_val=e * REGION * P, max_val=e * REGION * P + NT * P)
                sp.dma_start(routed[bass.ds(r, P), :], pad_rows[:]).then_inc(pad_out, 16)
            for s in range(SPARE):
                t0 = (E * REGION + s) * P
                sp.dma_start(routed[t0:t0 + P, :], pad_rows[:]).then_inc(pad_out, 16)
            sp.wait_ge(pad_out, 16 * (1 + E + SPARE))
            for done in x1_out:
                sp.wait_ge(done, 16 * B)

            def load_rows(t, u, q):
                if known(t, 4):
                    after(sp, (ey_done, t - 3), (eid_done, t - 3))
                r = sp.value_load(tblk_i[0:1, bass.ds(t, 1)], min_val=0, max_val=E * REGION + SPARE - 1)
                sp.dma_start(et[:, u], routed[bass.ds(r * P, P), :]).then_inc(et_in[u], 16)

            tiles(sp, load_rows)

        @block.gpsimd
        def _(gp):
            gp.dma_start(gates[:, 0:1], gx.to_broadcast([P, 1])).then_inc(gates_in, 16)
            gp.dma_start(gates[:, 1:2], gf.to_broadcast([P, 1])).then_inc(gates_in, 16)
            gp.dma_start(bfc_rows[:], bfc.rearrange("(o d) -> o d", o=1).to_broadcast([P, D])).then_inc(const_in, 16)
            with nc.allow_non_contiguous_dma(reason="biases, one word a partition"):
                for n, v in enumerate((bq, bk, bv)):
                    for a in range(DC):
                        gp.dma_start(bias[:, n, a:a + 1], v[a * P:(a + 1) * P].rearrange("(q o) -> q o", o=1)).then_inc(const_in, 16)
            gp.iota(head_i[:], [[P, CH], [-K2, H]], base=0, channel_multiplier=1).then_inc(iota_done, 1)
            gp.iota(own_i[:], [[-HD, HC]], base=0, channel_multiplier=1).then_inc(iota_done, 1)
            gp.iota(token_i[:], [[P, NT]], base=0, channel_multiplier=1).then_inc(iota_done, 1)
            gp.iota(expert_i[:], [[0, 2], [1, E]], base=0, channel_multiplier=0).then_inc(iota_done, 1)
            gp.iota(tile_i[:], [[1, MOE_T]], base=0, channel_multiplier=0).then_inc(iota_done, 1)
            gp.iota(pad_i[:], [[0, 1]], base=NT * P, channel_multiplier=1).then_inc(iota_done, 1)
            gp.memset(ident[:], 0.0).then_inc(iota_done, 1)
            gp.memset(upper[:], 1.0).then_inc(iota_done, 1)
            gp.wait_ge(iota_done, N_IOTA)
            gp.affine_select(out=ident[:], in_=ident[:], compare_op=ALU.not_equal, fill=1.0, base=0,
                             pattern=[[-1, P]], channel_multiplier=1).then_inc(ident_done, 1)
            gp.affine_select(out=upper[:], in_=upper[:], compare_op=ALU.is_gt, fill=0.0, base=0,
                             pattern=[[1, P]], channel_multiplier=-1).then_inc(ident_done, 1)

            def rstd_1(b):
                after(gp, (mvar1, QT * (b + 1)))
                gp.tensor_scalar(ve1[:], mv1[:, :, 1], EPS, 1.0, ALU.add, ALU.mult).then_inc(eps1, 1)
                gp.wait_ge(eps1, b + 1)
                gp.tensor_tensor(rs1[:], ve1[:], half_neg[:], ALU.pow).then_inc(rstd1, 1)

            def spread_keys(b, u):
                after(gp, *([(s_ps, QT * (b - 1))] if known(b, 2) else []))
                gp.tensor_copy(mrow[0:1, u], masked[0:1, bass.ds(b * K2, K2)]).then_inc(mrow_done, 1)
                gp.wait_ge(k_sb, DC * (b + 1))
                for c in range(DC):
                    gp.tensor_tensor(kbd[:, u, c], kT[:, c].rearrange("p (o k) -> p o k", o=1).to_broadcast([P, HC, K2]),
                                     own[:].rearrange("p (h o) -> p h o", o=1).to_broadcast([P, HC, K2]), ALU.mult).then_inc(kbd_done, 1)

            def residual(b, u, n):
                gp.wait_ge(x_in[u], 16 * (n + 1))
                if known(b, 2):
                    gp.wait_ge(x1_done, QT * (b - 1))
                for t in range(QT):
                    gp.tensor_tensor(xg[:, u, t], xb[:, u, t], bfc_rows[:], ALU.add).then_inc(xg_done, 1)

            gp.wait_ge(dv_const, 2)
            rstd_1(0)
            rstd_1(1)
            spread_keys(0, 0)
            residual(0, 0, 0)
            spread_keys(1, 1)

            def rstd_2(i):
                after(gp, (mvar2, i + 1))
                gp.tensor_scalar(ve2[:], mv2[:, 1:2], EPS, 1.0, ALU.add, ALU.mult).then_inc(eps2, 1)
                gp.wait_ge(eps2, i + 1)
                gp.tensor_tensor(rs2[:], ve2[:], half_neg[:, 0:1], ALU.pow).then_inc(rstd2, 1)

            def number_rows(i, u4):
                after(gp, (xn2_done, i + 1))
                gp.tensor_copy(rows[:, u4, :, D], token_id[:, bass.ds(i, 1)].to_broadcast([P, TOP_K])).then_inc(row_id, 1)

            def scatter(i, u4):
                after(gp, (slot_done, i + 1), (w_done, i + 1), (row_copy, i + 1), (row_id, i + 1))
                for k in range(TOP_K):
                    gp.indirect_dma_start(out=routed, out_offset=bass.IndirectOffsetOnAxis(ap=slot[:, u4, k:k + 1], axis=0),
                                          in_=rows[:, u4, k, :], in_offset=None).then_inc(scattered[u4], 16)

            def batch(b, u, n):
                for t in range(QT):
                    i = b * QT + t
                    u4 = u * QT + t
                    if known(i, 1):
                        rstd_2(i - 1)
                    if t == 0 and below(b, B - 1):
                        residual(b + 1, 1 - u, n + u)
                    if t == 1 and below(b, B - 2):
                        rstd_1(b + 2)
                    if known(i, 1):
                        number_rows(i - 1, (u4 - 1) % 4)
                    if known(i, 3):
                        scatter(i - 3, (u4 - 3) % 4)
                    if t == 1 and below(b, B - 2):
                        spread_keys(b + 2, u)

            batches(gp, batch)
            rstd_2(NT - 1)
            number_rows(NT - 1, 3)
            for i in range(NT - 3, NT):
                scatter(i, i % 4)

            def add_rows(t, u, q):
                after(gp, (ey_done, t + 1), (eid_done, t + 1), *([(added, 16 * t)] if known(t, 1) else []))
                gp.indirect_dma_start(out=out, out_offset=bass.IndirectOffsetOnAxis(ap=eid[:, u:u + 1], axis=0),
                                      in_=ey[:, u % 2, :], in_offset=None, compute_op=ALU.add).then_inc(added, 16)

            for done in x1_out:
                gp.wait_ge(done, 16 * B)
            gp.wait_ge(pad_out, 16 * (1 + E + SPARE))
            tiles(gp, add_rows)
            gp.wait_ge(added, 16 * MOE_T)

        @block.scalar
        def _(act):
            act.wait_ge(gates_in, 32)
            act.activation(tanhg[:], gates[:], ACT.Tanh).then_inc(tanh_done, 1)
            for n, name in enumerate(("wk", "wq", "wv", "wfc")):
                act.wait_ge(wT_ps, n + 1)
                act.copy(wT[name][:].rearrange("p c d -> p (c d)"), banks4[:, n]).then_inc(wT_sb, 1)
            act.wait_ge(const_in, 16 * CONST_LOADS)

            def ctx_evac(b):
                act.wait_ge(ctxT_ps, b + 1)
                if known(b, 1):
                    act.wait_ge(v_ps, b)
                for c in range(DC):
                    src = psK[:, c * K2:(c + 1) * K2].rearrange("p (o k) -> p o k", o=1).to_broadcast([P, 3, K2])
                    act.copy(ctxT[:, c], src).then_inc(ctxT_sb, 1)

            def x_evac(b):
                act.wait_ge(xT_ps, b + 1)
                act.copy(xnT[:].rearrange("p c s -> p (c s)"), psA[:]).then_inc(xT_sb, 1)

            def q_evac(b, u):
                act.wait_ge(q_ps, b + 1)
                for a in range(DC):
                    act.activation(qT[:, u, a], psA[:, a * S:(a + 1) * S], ACT.Identity, bias=bias[:, 0, a:a + 1]).then_inc(q_sb, 1)

            def t_evac(i, g):
                c0, c1 = T_GROUPS[g]
                act.wait_ge(t_ps, 3 * i + g + 1)
                if known(i, 1) and g == 0:
                    act.wait_ge(o_ps, i)
                act.copy(probT[:, c0:c1].rearrange("p c q -> p (c q)"), psT[:, 0:(c1 - c0) * P]).then_inc(t_sb, 1)

            def exp_scores(i, t):
                act.wait_ge(s_sub, 2 * (i + 1))
                act.activation(prob[:, t, 0:HK], prob[:, t, 0:HK], ACT.Exp, scale=scale).then_inc(p_done, 1)

            def n2_evac(i):
                act.wait_ge(n2T_ps, i + 1)
                act.copy(xn2T[:].rearrange("p c q -> p (c q)"), psG[:, 0:D]).then_inc(n2T_sb, 1)

            def exp_gap(i):
                act.wait_ge(gap_done, i + 1)
                act.activation(egap[:], gap[:], ACT.Exp).then_inc(egap_done, 1)

            def o_evac(i):
                act.wait_ge(oT_ps, i + 1)
                for c in range(DC):
                    act.activation(onT[:, c], psB[:, c * P:(c + 1) * P], ACT.Identity, bias=bias[:, 2, c:c + 1]).then_inc(oT_sb, 1)

            def copy_row(i, u4):
                act.wait_ge(xn2_done, i + 1)
                act.copy(rows[:, u4, 1, 0:D], rows[:, u4, 0, 0:D]).then_inc(row_copy, 1)

            ctx_evac(0)
            x_evac(0)
            q_evac(0, 0)
            ctx_evac(1)
            exp_scores(0, 0)

            def batch(b, u, n):
                for t in range(QT):
                    i = b * QT + t
                    u4 = u * QT + t
                    if known(i, 1):
                        o_evac(i - 1)
                    t_evac(i, 0)
                    if known(i, 2):
                        n2_evac(i - 2)
                    t_evac(i, 1)
                    if t == 0 and below(b, B - 1):
                        x_evac(b + 1)
                    t_evac(i, 2)
                    if known(i, 2):
                        exp_gap(i - 2)
                    if t == 0 and below(b, B - 1):
                        q_evac(b + 1, 1 - u)
                    if t == 1 and below(b, B - 2):
                        ctx_evac(b + 2)
                    if t == 0 or below(b, B - 1):
                        exp_scores(i + 1, 1 - t)
                    if known(i, 1):
                        copy_row(i - 1, (u4 - 1) % 4)

            batches(act, batch)
            o_evac(NT - 1)
            n2_evac(NT - 2)
            exp_gap(NT - 2)
            copy_row(NT - 1, 3)
            n2_evac(NT - 1)
            exp_gap(NT - 1)

            def e_evac(t, u):
                act.wait_ge(etT_ps, t + 1)
                act.copy(etT[:, u % 2].rearrange("p c q -> p (c q)"), psG[:, 0:D]).then_inc(etT_sb, 1)

            def silu(t, u):
                act.wait_ge(h0_ps, t + 1)
                if known(t, 2):
                    act.wait_ge(hg_done, t - 1)
                act.activation(hs[:, u % 2], banks4[:, u % 2], ACT.Silu).then_inc(hs_done, 1)

            def y_evac(t, u):
                act.wait_ge(ey_ps, t + 1)
                if known(t, 2):
                    act.wait_ge(added, 16 * (t - 1))
                act.activation(ey[:, u % 2], psB[:, 0:D], ACT.Copy, scale=et[:, u, D + 1:D + 2]).then_inc(ey_done, 1)

            e_evac(0, 0)

            def tile(t, u, q):
                if below(t, MOE_T - 1):
                    e_evac(t + 1, u + 1)
                silu(t, u)
                if known(t, 1):
                    y_evac(t - 1, (u - 1) % 4)

            tiles(act, tile)
            y_evac(MOE_T - 1, 3)

        @block.vector
        def _(dve):
            dve.memset(pad_rows[:, 0:D], 0.0).then_inc(dv_const, 1)
            dve.memset(pad_rows[:, D + 1:D + 2], 0.0).then_inc(valid_done, 1)
            dve.memset(half_neg[:], -0.5).then_inc(valid_done, 1)
            dve.memset(ones[:], 1.0).then_inc(valid_done, 1)
            dve.memset(one_e[:], 1.0).then_inc(valid_done, 1)
            dve.wait_ge(iota_done, N_IOTA)
            dve.tensor_copy(pad_rows[:, D:D + 1], pad_i[:]).then_inc(valid_done, 1)
            dve.tensor_copy(token_id[:], token_i[:]).then_inc(valid_done, 1)
            dve.tensor_copy(expert_f[:], expert_i[:]).then_inc(valid_done, 1)
            dve.tensor_copy(tile_f[:], tile_i[:]).then_inc(valid_done, 1)
            dve.tensor_copy(head_f[:], head_i[:]).then_inc(valid_done, 1)
            dve.tensor_copy(own_f[:], own_i[:]).then_inc(valid_done, 1)
            dve.wait_ge(valid_done, 10)
            dve.tensor_scalar(head_lt[:], head_f[:], K2 - 0.5, None, ALU.is_lt).then_inc(valid_done, 1)
            dve.tensor_scalar(own_lt[:], own_f[:], HD - 0.5, None, ALU.is_lt).then_inc(valid_done, 1)
            dve.tensor_scalar(region0[:], expert_f[:, 0], float(REGION * P), None, ALU.mult).then_inc(valid_done, 1)
            dve.tensor_scalar(base[:], expert_f[:, 0], float(REGION * P), None, ALU.mult).then_inc(valid_done, 1)
            dve.wait_ge(valid_done, 14)
            dve.scalar_tensor_tensor(out=own[:], in0=own_f[:], scalar=-0.5, in1=own_lt[:], op0=ALU.is_gt, op1=ALU.mult).then_inc(valid_done, 1)
            dve.scalar_tensor_tensor(out=head_f[:], in0=head_f[:], scalar=-0.5, in1=head_lt[:], op0=ALU.is_gt, op1=ALU.mult).then_inc(valid_done, 1)
            dve.wait_ge(valid_done, 16)
            for c in range(CH):
                dve.tensor_copy(head_of[:, c], head_f[:, c, first_head[c]:first_head[c] + 3]).then_inc(valid_done, 1)
            dve.wait_ge(valid_done, 16 + CH)
            for u in range(2):
                dve.tensor_copy(vbd[:, u, :, :, HD], head_of[:]).then_inc(valid_done, 1)
            dve.wait_ge(mask_in, 16)
            dve.tensor_scalar(valid[:], mask_sb, 0, None, ALU.not_equal).then_inc(valid_done, 1)
            dve.tensor_scalar(masked[:], mask_sb, 0, MASKED / scale, ALU.is_equal, ALU.mult).then_inc(valid_done, 1)
            dve.wait_ge(const_in, 16 * CONST_LOADS)
            dve.wait_ge(tanh_done, 1)
            dve.tensor_scalar(bfc_rows[:], bfc_rows[:], tanhg[:, 0:1], None, ALU.mult).then_inc(valid_done, 1)
            dve.wait_ge(valid_done, 21 + CH)
            dve.memset(prob[:, :, HK:CH * P], 0.0).then_inc(valid_done, 1)
            dve.wait_ge(valid_done, 22 + CH)
            dve.engine_nop().then_inc(dv_const, 1)

            def stats_1(b, u, n):
                dve.wait_ge(x_in[u], 16 * (n + 1))
                if known(b, 1):
                    dve.wait_ge(rstd1, b)
                for t in range(QT):
                    dve.bn_stats(st1[:, t], xb[:, u, t]).then_inc(stat1, 1)
                after(dve, (stat1, QT * (b + 1)))
                for t in range(QT):
                    dve.bn_aggr(mv1[:, t], st1[:, t]).then_inc(mvar1, 1)

            def norm_1(b, u):
                dve.wait_ge(rstd1, b + 1)
                dve.wait_ge(mvar1, QT * (b + 1))
                if known(b, 1):
                    dve.wait_ge(xT_ps, b)
                for t in range(QT):
                    m = dve.tensor_scalar(xn[:, t], xb[:, u, t], mv1[:, t, 0:1], rs1[:, t:t + 1], ALU.subtract, ALU.mult)
                m.then_inc(xn_done, 1)

            def k_evac(b):
                dve.wait_ge(k_ps, b + 1)
                if known(b, 1):
                    dve.wait_ge(kbd_done, DC * b)
                for a in range(DC):
                    dve.scalar_tensor_tensor(out=kT[:, a], in0=psK[:, a * K2:(a + 1) * K2], scalar=bias[:, 1, a:a + 1],
                                             in1=valid[:, bass.ds(b * K2, K2)], op0=ALU.add, op1=ALU.mult).then_inc(k_sb, 1)

            def v_evac(b, u):
                dve.wait_ge(v_ps, b + 1)
                dve.tensor_tensor(vbd[:, u, :, :, 0:HD].rearrange("p c h d -> p (c h) d"),
                                  psA[:, 0:CH * 3 * HD].rearrange("p (n d) -> p n d", d=HD),
                                  head_of[:].rearrange("p c (h o) -> p (c h) o", o=1).to_broadcast([P, CH * 3, HD]), ALU.mult).then_inc(v_sb, 1)

            def softmax_shift(i, t):
                dve.wait_ge(s_ps, i + 1)
                split = S_FULL * HB
                parts = [(psS[:, 0:S_FULL, 0:HB * K2].rearrange("p n (h k) -> p n h k", k=K2), 0, S_FULL, HB),
                         (psS[:, S_FULL:S_FULL + 1, 0:(H - split) * K2].rearrange("p n (h k) -> p n h k", k=K2), split, 1, H - split)]
                for sv, h0, n, k in parts:
                    dve.tensor_reduce(mx[:, t, h0:h0 + n * k].rearrange("p (n h) -> p n h", n=n), sv, AX_X, ALU.max).then_inc(s_max, 1)
                dve.wait_ge(s_max, 2 * (i + 1))
                for sv, h0, n, k in parts:
                    dve.tensor_tensor(prob[:, t, h0 * K2:(h0 + n * k) * K2].rearrange("p (n h k) -> p n h k", n=n, k=K2), sv,
                                      mx[:, t, h0:h0 + n * k].rearrange("p (n h o) -> p n h o", n=n, o=1).to_broadcast([P, n, k, K2]),
                                      ALU.subtract).then_inc(s_sub, 1)

            def o_norm(i):
                dve.wait_ge(o_ps, i + 1)
                ov = psB[:, 0:H * VW].rearrange("p (h d) -> p h d", d=VW)
                dve.reciprocal(rden[:], ov[:, :, HD]).then_inc(o_rec, 1)
                dve.wait_ge(o_rec, i + 1)
                dve.tensor_tensor(on[:].rearrange("p (h d) -> p h d", d=HD), ov[:, :, 0:HD],
                                  rden[:].rearrange("p (h o) -> p h o", o=1).to_broadcast([P, H, HD]), ALU.mult).then_inc(o_sb, 1)

            def residual_1(i, u, t, b):
                dve.wait_ge(y_ps, i + 1)
                dve.wait_ge(xg_done, QT * (b + 1))
                if known(b, 1):
                    dve.wait_ge(x1_out[t], 16 * b)
                dve.scalar_tensor_tensor(out=x1[:, t], in0=psB[:, 0:D], scalar=tanhg[:, 0:1], in1=xg[:, u, t], op0=ALU.mult, op1=ALU.add).then_inc(x1_done, 1)
                dve.wait_ge(x1_done, i + 1)
                dve.bn_stats(st2[:], x1[:, t]).then_inc(stat2, 1)
                after(dve, (stat2, i + 1))
                dve.bn_aggr(mv2[:], st2[:]).then_inc(mvar2, 1)

            def norm_2(i, t, u4, n):
                dve.wait_ge(rstd2, i + 1)
                dve.wait_ge(mvar2, i + 1)
                if known(n, 1):
                    dve.wait_ge(scattered[u4], 32 * n)
                dve.tensor_scalar(rows[:, u4, 0, 0:D], x1[:, t], mv2[:, 0:1], rs2[:, 0:1], ALU.subtract, ALU.mult).then_inc(xn2_done, 1)

            def choose(i):
                dve.wait_ge(g_ps, i + 1)
                dve.tensor_copy(logit[:], psG[:, D:D + E]).then_inc(l_cp, 1)
                after(dve, (l_cp, i + 1))
                dve.max(top[:], logit[:]).then_inc(l_max, 1)
                after(dve, (l_max, i + 1))
                dve.max_index(topi[:], top[:], logit[:]).then_inc(l_idx, 1)
                if known(i, 1):
                    dve.wait_ge(egap_done, i)
                dve.tensor_tensor(gap[:], top[:, 1:2], top[:, 0:1], ALU.subtract).then_inc(gap_done, 1)
                dve.wait_ge(l_idx, i + 1)
                dve.tensor_copy(topf[:], topi[:, 0:TOP_K]).then_inc(l_idf, 1)
                dve.wait_ge(l_idf, i + 1)
                dve.tensor_tensor(chosen[:], expert_f[:], topf[:].rearrange("p (k o) -> p k o", o=1).to_broadcast([P, TOP_K, E]), ALU.is_equal).then_inc(l_oh, 1)
                dve.wait_ge(l_oh, i + 1)
                dve.tensor_tensor(chosen_any[:], chosen[:, 0], chosen[:, 1], ALU.add).then_inc(l_any, 1)

            def place(i, u4):
                dve.wait_ge(r_ps, i + 1)
                dve.tensor_tensor(pos[:], psG[:, D + E:D + 2 * E], base[:], ALU.add).then_inc(pos_done, 1)
                dve.wait_ge(egap_done, i + 1)
                dve.tensor_scalar(wsum[:], egap[:], 1.0, None, ALU.add).then_inc(w_sum, 1)
                dve.wait_ge(pos_done, i + 1)
                dve.tensor_tensor(base[:], psG[:, D + 2 * E:D + 3 * E], base[:], ALU.add).then_inc(base_done, 1)
                dve.tensor_tensor(picked[:], chosen[:], pos[:].rearrange("p (o e) -> p o e", o=1).to_broadcast([P, TOP_K, E]), ALU.mult).then_inc(pick_done, 1)
                dve.wait_ge(w_sum, i + 1)
                dve.reciprocal(wrec[:], wsum[:]).then_inc(w_rec, 1)
                dve.wait_ge(pick_done, i + 1)
                dve.tensor_reduce(slotf[:], picked[:], AX_X, ALU.add).then_inc(slotf_done, 1)
                dve.wait_ge(w_rec, i + 1)
                dve.tensor_tensor(rows[:, u4, 0, D + 1:D + 2], wrec[:], tanhg[:, 1:2], ALU.mult).then_inc(w_one, 1)
                dve.wait_ge(slotf_done, i + 1)
                dve.tensor_copy(slot[:, u4], slotf[:]).then_inc(slot_done, 1)
                dve.wait_ge(w_one, i + 1)
                dve.tensor_tensor(rows[:, u4, 1, D + 1:D + 2], rows[:, u4, 0, D + 1:D + 2], egap[:], ALU.mult).then_inc(w_done, 1)
                dve.wait_ge(base_done, i + 1)

            stats_1(0, 0, 0)
            norm_1(0, 0)
            stats_1(1, 1, 0)
            k_evac(0)
            norm_1(1, 1)
            v_evac(0, 0)
            k_evac(1)
            softmax_shift(0, 0)

            def batch(b, u, n):
                for t in range(QT):
                    i = b * QT + t
                    u4 = u * QT + t
                    if t == 0 or below(b, B - 1):
                        softmax_shift(i + 1, 1 - t)
                    if known(i, 1):
                        residual_1(i - 1, u if t else 1 - u, 1 - t, b if t else b - 1)
                    if known(i, 2):
                        choose(i - 2)
                    if t == 1 and below(b, B - 1):
                        v_evac(b + 1, 1 - u)
                    if t == 1 and below(b, B - 2):
                        stats_1(b + 2, u, n + 1)
                    if known(i, 1):
                        norm_2(i - 1, 1 - t, (u4 - 1) % 4, n if u4 else n - 1)
                    o_norm(i)
                    if known(i, 2):
                        place(i - 2, (u4 - 2) % 4)
                    if t == 1 and below(b, B - 2):
                        k_evac(b + 2)
                        norm_1(b + 2, u)

            batches(dve, batch)
            residual_1(NT - 1, 1, 1, B - 1)
            choose(NT - 2)
            norm_2(NT - 1, 1, 3, LOOPS - 1)
            place(NT - 2, 2)
            choose(NT - 1)
            place(NT - 1, 3)

            steps = [0]

            def step(m):
                m.then_inc(tab, 1)
                steps[0] += 1
                dve.wait_ge(tab, steps[0])

            step(dve.tensor_copy(base_i[:], base[:]))
            step(dve.tensor_tensor(cnt_f[:], base[:], region0[:], ALU.subtract))
            step(dve.tensor_scalar(cnt_f[:], cnt_f[:], float(P - 1), None, ALU.add))
            step(dve.tensor_copy(cnt_i[:], cnt_f[:]))
            step(dve.tensor_scalar(nt_i[:], cnt_i[:], P.bit_length() - 1, None, ALU.logical_shift_right))
            step(dve.tensor_copy(nt_f[:], nt_i[:]))
            step(dve.tensor_tensor_scan(tend[:], one_e[:], nt_f[:], 0.0, ALU.mult, ALU.add))
            step(dve.tensor_scalar(skip[:], nt_f[:], -1.0, float(REGION), ALU.mult, ALU.add))
            step(dve.tensor_tensor(past[:], tile_f[:].rearrange("p (t o) -> p t o", o=1).to_broadcast([P, MOE_T, E]),
                                   tend[:].rearrange("p (o e) -> p o e", o=1).to_broadcast([P, MOE_T, E]), ALU.is_ge))
            step(dve.tensor_reduce(texp[:], past[:], AX_X, ALU.add))
            step(dve.tensor_scalar(texp2[:], texp[:], float(E - 1), None, ALU.min))
            step(dve.tensor_copy(texp_i[:], texp2[:]))
            step(dve.tensor_tensor(past[:], past[:], skip[:].rearrange("p (o e) -> p o e", o=1).to_broadcast([P, MOE_T, E]), ALU.mult))
            step(dve.tensor_reduce(tblk[:], past[:], AX_X, ALU.add))
            step(dve.tensor_tensor(tblk[:], tblk[:], tile_f[:], ALU.add))
            step(dve.tensor_copy(tblk_i[:], tblk[:]))
            dve.engine_nop().then_inc(tab_done, 1)

            def glu(t, u):
                dve.wait_ge(h1_ps, t + 1)
                dve.wait_ge(hs_done, t + 1)
                if known(t, 2):
                    dve.wait_ge(hgT_ps, t - 1)
                dve.tensor_tensor(hg[:, u % 2], banks4[:, 2 + u % 2], hs[:, u % 2], ALU.mult).then_inc(hg_done, 1)

            def g_evac(t, u):
                dve.wait_ge(hgT_ps, t + 1)
                if known(t, 2):
                    dve.wait_ge(ey_ps, t - 1)
                dve.tensor_copy(hgT[:, u % 2].rearrange("p c q -> p (c q)"), psT[:]).then_inc(hgT_sb, 1)

            def tile(t, u, q):
                dve.wait_ge(et_in[u], 16 * (q + 1))
                if known(t, 4):
                    dve.wait_ge(added, 16 * (t - 3))
                dve.tensor_copy(eid[:, u:u + 1], et[:, u, D:D + 1]).then_inc(eid_done, 1)
                if known(t, 1):
                    g_evac(t - 1, (u - 1) % 4)
                glu(t, u)

            tiles(dve, tile)
            g_evac(MOE_T - 1, 3)

        @block.tensor
        def _(pe):
            pe.wait_ge(ident_done, 2)
            pe.wait_ge(raw_in, 16 * 4)
            for n in range(4):
                for c in range(DC):
                    for o in range(DC):
                        m = pe.transpose(banks4[:, n, (c * DC + o) * P:(c * DC + o + 1) * P], raw[:, n, o, c * P:(c + 1) * P], ident[:])
                m.then_inc(wT_ps, 1)

            def ctx_T(b, u, n):
                pe.wait_ge(ctx_in_s[u], 16 * (n + 1))
                if known(b, 1):
                    pe.wait_ge(k_sb, DC * b)
                for c in range(DC):
                    m = pe.transpose(psK[:, c * K2:(c + 1) * K2], cb[:, u, c * P:(c + 1) * P], ident[0:K2, 0:K2])
                m.then_inc(ctxT_ps, 1)

            def keys(b):
                pe.wait_ge(ctxT_sb, DC * (b + 1))
                for a in range(2):
                    for c in range(DC):
                        m = pe.matmul(psK[:, a * K2:(a + 1) * K2], wT["wk"][:, c, a * P:(a + 1) * P], ctxT[:, c, 0], start=(c == 0), stop=(c == DC - 1))
                m.then_inc(k_ps, 1)

            def x_T(b):
                pe.wait_ge(xn_done, b + 1)
                if known(b, 1):
                    pe.wait_ge(v_sb, b)
                for c in range(DC):
                    for t in range(QT):
                        m = pe.transpose(psA[:, c * S + t * P:c * S + (t + 1) * P], xn[:, t, c * P:(c + 1) * P], ident[:])
                m.then_inc(xT_ps, 1)

            def queries(b):
                pe.wait_ge(xT_sb, b + 1)
                for a in range(2):
                    for c in range(DC):
                        m = pe.matmul(psA[:, a * S:(a + 1) * S], wT["wq"][:, c, a * P:(a + 1) * P], xnT[:, c], start=(c == 0), stop=(c == DC - 1))
                m.then_inc(q_ps, 1)

            def values(b, part):
                if part == 0:
                    pe.wait_ge(q_sb, DC * (b + 1))
                half = CH // 2
                for j in range(half * part, half * part + half if part == 0 else CH):
                    s = P * j % K2
                    h = first_head[j]
                    for c in range(DC):
                        lhsT = ctxT[:, c].rearrange("p o k -> p (o k)")[:, s:s + P]
                        m = pe.matmul(psA[:, j * 3 * HD:(j + 1) * 3 * HD], lhsT, wT["wv"][:, c, h * HD:(h + 3) * HD], start=(c == 0), stop=(c == DC - 1))
                if part == 1:
                    m.then_inc(v_ps, 1)

            def scores(i, u, t, b):
                pe.wait_ge(q_sb, DC * (b + 1))
                pe.wait_ge(kbd_done, DC * (b + 1))
                pe.wait_ge(mrow_done, b + 1)
                if known(i, 1):
                    pe.wait_ge(s_sub, 2 * i)
                for n, h, k in S_BANKS:
                    pe.matmul(psS[:, n, 0:k * K2], ones[0:1, :], mrow[0:1, u].rearrange("p (o k) -> p o k", o=1).to_broadcast([1, k, K2]),
                              start=True, stop=False, skip_group_check=True)
                for n, c, h0, h1 in S_PIECES:
                    first = S_BANKS[n][1]
                    m = pe.matmul(psS[:, n, (h0 - first) * K2:(h1 - first) * K2], qT[:, u, c, t * P:(t + 1) * P],
                                  kbd[:, u, c, h0 - c * HC:h1 - c * HC].rearrange("p h k -> p (h k)"),
                                  start=False, stop=True, skip_group_check=True)
                m.then_inc(s_ps, 1)

            def prob_T(i, t, g):
                c0, c1 = T_GROUPS[g]
                if g == 0:
                    pe.wait_ge(p_done, i + 1)
                if known(3 * i + g, 1):
                    pe.wait_ge(t_sb, 3 * i + g)
                for c in range(c0, c1):
                    m = pe.transpose(psT[:, (c - c0) * P:(c - c0 + 1) * P], prob[:, t, c * P:(c + 1) * P], ident[:])
                m.then_inc(t_ps, 1)

            def attend(i, u, b):
                pe.wait_ge(t_sb, 3 * (i + 1))
                pe.wait_ge(v_sb, b + 1)
                if known(i, 1):
                    pe.wait_ge(x1_done, i)
                for c in range(CH):
                    h = first_head[c]
                    m = pe.matmul(psB[:, h * VW:(h + 3) * VW], probT[:, c], vbd[:, u, c].rearrange("p h d -> p (h d)"),
                                  start=(c == 0), stop=(c == CH - 1), skip_group_check=True)
                m.then_inc(o_ps, 1)

            def o_T(i):
                pe.wait_ge(o_sb, i + 1)
                for c in range(DC):
                    m = pe.transpose(psB[:, c * P:(c + 1) * P], on[:, c * P:(c + 1) * P], ident[:])
                m.then_inc(oT_ps, 1)

            def project(i):
                pe.wait_ge(oT_sb, DC * (i + 1))
                for c in range(DC):
                    m = pe.matmul(psB[:, 0:D], onT[:, c], wT["wfc"][:, c], start=(c == 0), stop=(c == DC - 1))
                m.then_inc(y_ps, 1)

            def n2_T(i, u4):
                pe.wait_ge(xn2_done, i + 1)
                if known(i, 1):
                    pe.wait_ge(base_done, i)
                for c in range(DC):
                    m = pe.transpose(psG[:, c * P:(c + 1) * P], rows[:, u4, 0, c * P:(c + 1) * P], ident[:])
                m.then_inc(n2T_ps, 1)

            def gate(i):
                pe.wait_ge(n2T_sb, i + 1)
                for c in range(DC):
                    m = pe.matmul(psG[:, D:D + E], xn2T[:, c], gate_sb[:, c], start=(c == 0), stop=(c == DC - 1))
                m.then_inc(g_ps, 1)

            def rank(i):
                pe.wait_ge(l_any, i + 1)
                pe.matmul(psG[:, D + E:D + 2 * E], upper[:], chosen_any[:], start=True, stop=True)
                pe.matmul(psG[:, D + 2 * E:D + 3 * E], ones[:], chosen_any[:], start=True, stop=True).then_inc(r_ps, 1)

            pe.wait_ge(wT_sb, 4)
            pe.wait_ge(dv_const, 2)
            pe.wait_ge(gate_in, 16)
            ctx_T(0, 0, 0)
            x_T(0)
            keys(0)
            queries(0)
            values(0, 0)
            values(0, 1)
            ctx_T(1, 1, 0)
            scores(0, 0, 0, 0)
            keys(1)
            scores(1, 0, 1, 0)

            def batch(b, u, n):
                more = below(b, B - 1)
                for t in range(QT):
                    i = b * QT + t
                    u4 = u * QT + t
                    if known(i, 1):
                        o_T(i - 1)
                    prob_T(i, t, 0)
                    if known(i, 2):
                        n2_T(i - 2, (u4 - 2) % 4)
                    if known(i, 1):
                        project(i - 1)
                    prob_T(i, t, 1)
                    if more:
                        x_T(b + 1) if t == 0 else values(b + 1, 0)
                    if known(i, 2):
                        gate(i - 2)
                    prob_T(i, t, 2)
                    if more:
                        queries(b + 1) if t == 0 else values(b + 1, 1)
                    if t == 1 and below(b, B - 2):
                        ctx_T(b + 2, u, n + 1)
                    attend(i, u, b)
                    if known(i, 2):
                        rank(i - 2)
                    if t == 1 and below(b, B - 2):
                        keys(b + 2)
                    if more:
                        scores(i + 2, 1 - u, t, b + 1)

            batches(pe, batch)
            o_T(NT - 1)
            n2_T(NT - 2, 2)
            project(NT - 1)
            gate(NT - 2)
            rank(NT - 2)
            n2_T(NT - 1, 3)
            gate(NT - 1)
            rank(NT - 1)

            pe.wait_ge(moe_in, 16 * 3 * E)
            pe.wait_ge(tab_done, 1)

            def e_T(t, u, q):
                pe.wait_ge(et_in[u], 16 * (q + 1))
                if known(t, 1):
                    pe.wait_ge(etT_sb, t)
                for c in range(DC):
                    m = pe.transpose(psG[:, c * P:(c + 1) * P], et[:, u, c * P:(c + 1) * P], ident[:])
                m.then_inc(etT_ps, 1)

            def up(t, u, e, w, bank, done):
                for c in range(DC):
                    m = pe.matmul(banks4[:, bank], etT[:, u % 2, c], w[:].rearrange("p e c f -> p (e c) f")[:, bass.ds(e * DC + c, 1), :].rearrange("p o f -> p (o f)"),
                                  start=(c == 0), stop=(c == DC - 1))
                m.then_inc(done, 1)

            def g_T(t, u):
                pe.wait_ge(hg_done, t + 1)
                if known(t, 1):
                    pe.wait_ge(hgT_sb, t)
                for c in range(FC):
                    m = pe.transpose(psT[:, c * P:(c + 1) * P], hg[:, u % 2, c * P:(c + 1) * P], ident[:])
                m.then_inc(hgT_ps, 1)

            def down(t, u, e):
                pe.wait_ge(hgT_sb, t + 1)
                if known(t, 1):
                    pe.wait_ge(ey_done, t)
                for c in range(FC):
                    m = pe.matmul(psB[:, 0:D], hgT[:, u % 2, c], wo_sb[:].rearrange("p e c d -> p (e c) d")[:, bass.ds(e * FC + c, 1), :].rearrange("p o d -> p (o d)"),
                                  start=(c == 0), stop=(c == FC - 1))
                m.then_inc(ey_ps, 1)

            def expert_of(t):
                return pe.value_load(texp_i[0:1, bass.ds(t, 1)], min_val=0, max_val=E - 1)

            e_T(0, 0, 0)

            def tile(t, u, q):
                e = expert_of(t)
                pe.wait_ge(etT_sb, t + 1)
                if known(t, 2):
                    pe.wait_ge(hg_done, t - 1)
                up(t, u, e, w0_sb, u % 2, h0_ps)
                if known(t, 1):
                    g_T(t - 1, (u - 1) % 4)
                if below(t, MOE_T - 1):
                    e_T(t + 1, (u + 1) % 4, q + (u == 3))
                up(t, u, e, w1_sb, 2 + u % 2, h1_ps)
                if known(t, 1):
                    down(t - 1, (u - 1) % 4, expert_of(t - 1))

            tiles(pe, tile)
            g_T(MOE_T - 1, 3)
            down(MOE_T - 1, 3, expert_of(MOE_T - 1))


_INS = ["x", "ctx_1024", "mask_BxS2_ik0", "g_xattn", "g_ffn",
        "L0_xattn_Wq", "L0_xattn_bq", "L0_xattn_Wk", "L0_xattn_bk", "L0_xattn_Wv", "L0_xattn_bv",
        "L0_xattn_Wfc", "L0_xattn_bfc", "L0_ffn_gate_kernel", "L0_ffn_w0_kernel", "L0_ffn_w1_kernel",
        "L0_ffn_wo_kernel"]


def kernel(**inputs):
    import numpy as _np
    import concourse.bacc as _bacc
    from concourse import mybir as _mybir
    from concourse.bass_utils import run_bass_kernel_spmd as _run

    nc = _bacc.Bacc("TRN2", target_bir_lowering=False, num_devices=1)
    arrays, args = {}, []
    for name in _INS:
        a = _np.ascontiguousarray(inputs[name])
        arrays[f"in_{name}_dram"] = a
        args.append(nc.dram_tensor(f"in_{name}_dram", a.shape, _mybir.dt.from_np(a.dtype), kind="ExternalInput").ap())
    B, S, D = inputs["x"].shape
    args.append(nc.dram_tensor("out_0_dram", (B * S + P, D), F32, kind="ExternalOutput").ap())
    flamingo_gated_layer(nc, *args)
    r = _run(nc, [arrays], core_ids=[0])
    return r.results[0]["out_0_dram"][:B * S].reshape(B, S, D)
```

```python
from contextlib import ExitStack

import concourse.bass as bass
from concourse import mybir

F32 = mybir.dt.float32
BF16 = mybir.dt.bfloat16
F32R = mybir.dt.float32r
I32 = mybir.dt.int32
U32 = mybir.dt.uint32
ALU = mybir.AluOpType
ACT = mybir.ActivationFunctionType
AX_X = mybir.AxisListType.X

P = 128
EPS = 1e-5
MASKED = -1e10
TOP_K = 2
ROW = 2


def flamingo_gated_layer(nc, x, ctx_in, mask, g_xattn, g_ffn, Wq, bq, Wk, bk, Wv, bv, Wfc, bfc,
                         gate_kernel, w0, w1, wo, out):
    B, S, D = x.shape
    K2 = ctx_in.shape[1]
    HD = 16
    H = D // HD
    QT = S // P
    NT = B * QT
    DC = D // P
    E, _, F = w0.shape
    FC = F // P
    scale = float(HD) ** -0.5
    assert QT == 2 and DC == 2 and B % 4 == 0

    HB = 512 // K2
    HC = P // HD
    S_BANKS = [(n, h, min(HB, H - h)) for n, h in enumerate(range(0, H, HB))]
    S_PIECES = [(n, c, max(h, c * HC), min(h + k, (c + 1) * HC)) for n, h, k in S_BANKS for c in range(DC)
                if max(h, c * HC) < min(h + k, (c + 1) * HC)]
    S_FULL = H // HB
    assert len(S_BANKS) == 3 and S_FULL == 2
    HK = H * K2
    CH = -(-HK // P)
    first_head = [min(P * c // K2, H - 3) for c in range(CH)]
    VW = HD + 1
    T_GROUPS = [(0, 4), (4, 8), (8, CH)]

    REGION = NT + 1
    MOE_T = NT * TOP_K + E - 1
    SPARE = MOE_T - NT * TOP_K
    RW = D + ROW
    routed = nc.dram_tensor("routed_rows", [(E * REGION + SPARE) * P, RW], F32, kind="Internal").ap()

    x_t = x.rearrange("b (t p) d -> b p t d", p=P)
    gx = g_xattn.rearrange("(o a) -> o a", o=1)
    gf = g_ffn.rearrange("(o a) -> o a", o=1)

    NQ = E * DC
    QW = 2 * F + FC // DC * D
    FR = QW // F
    assert FR == 3 and FC // DC * D == F and NQ == B // 2
    EARLY = 2 * DC
    split_w = nc.dram_tensor("split_weights", [NQ, P, 2 * QW], F32, kind="Internal").ap()

    with ExitStack() as ctx, ExitStack() as attention:
        memory = ctx

        def sb(name, shape, dt=F32):
            return memory.enter_context(nc.sbuf_tensor(name, shape, dt))

        def ps(name, shape, dt=F32):
            return ctx.enter_context(nc.psum_tensor(name, shape, dt))

        def sem(name):
            return ctx.enter_context(nc.semaphore(name))

        ident = sb("ident", [P, P])
        texp_i = sb("texp_i", [P, MOE_T], I32)
        tblk_i = sb("tblk_i", [P, MOE_T], I32)
        et = sb("et", [P, 2, RW])
        hs = sb("hs", [P, F])
        ey = sb("ey", [P, 2, D])
        eid = sb("eid", [P, 4], I32)
        ewt = sb("ewt", [P, 4])
        etT = sb("etT", [P, 2, 2, DC, P], F32R)
        hgT = sb("hgT", [P, 2, FC, P], F32R)

        memory = attention
        sb("early_weights", [P, EARLY * 2 * QW])
        w_raw = sb("w_raw", [P, FR, F])
        w_part = sb("w_part", [P, 2, FR, F], F32R)
        wT = {n: sb(f"{n}T", [P, DC, D]) for n in ("wk", "wq", "wv", "wfc")}
        gate_sb = sb("gate_sb", [P, DC, E])
        bias = sb("bias", [P, 3, DC])
        bfc_rows = sb("bfc_rows", [P, D])
        gates = sb("gates", [P, 2])
        tanhg = sb("tanhg", [P, 2])
        upper = sb("upper", [P, P], BF16)
        ones = sb("ones", [P, P], BF16)
        valid = sb("valid", [P, B * K2], BF16)
        masked = sb("masked", [P, B * K2], BF16)
        own_i = sb("own_i", [P, HC], I32)
        own_f = sb("own_f", [P, HC])
        own_lt = sb("own_lt", [P, HC])
        own = sb("own", [P, HC])
        pick_key = sb("pick_key", [K2, 3 * K2], BF16)
        head_i = sb("head_i", [P, CH, H], I32)
        head_f = sb("head_f", [P, CH, H])
        head_lt = sb("head_lt", [P, CH, H])
        head_of = sb("head_of", [P, CH, 3])
        token_id = sb("token_id", [P, NT])
        token_i = sb("token_i", [P, NT], I32)
        expert_i = sb("expert_i", [P, 2, E], I32)
        expert_f = sb("expert_f", [P, 2, E])
        half_neg = sb("half_neg", [P, 2])
        neg_one = sb("neg_one", [P, 1])
        region0 = sb("region0", [P, E])
        pad_rows = sb("pad_rows", [P, RW])
        pad_i = sb("pad_i", [P, 1], I32)

        xb = sb("xb", [P, 2, QT, D])
        xg = sb("xg", [P, 2, QT, D])
        cb = sb("cb", [K2, 2, D])
        xn = sb("xn", [P, QT, D])
        xnT = sb("xnT", [P, DC, S])
        ctxT = sb("ctxT", [P, DC, K2])
        vparts = sb("vparts", [K2, 3, D], BF16)
        vrest = sb("vrest", [K2, D])
        qT = sb("qT", [P, 2, 2, DC, S], F32R)
        kT = sb("kT", [P, DC, K2])
        kT2 = sb("kT2", [P, 2, DC, K2], F32R)
        kbd = sb("kbd", [P, 2, 2, DC, HC, K2], F32R)
        share = sb("share", [P, P], BF16)
        mrow = sb("mrow", [P, 2, K2], BF16)
        vbd = sb("vbd", [P, 2, CH, 3, VW])
        prob = sb("prob", [P, 2, CH * P])
        probT = sb("probT", [P, CH, P])
        mx = sb("mx", [P, 2, H])
        neg_mx = sb("neg_mx", [P, 2, H - S_FULL * HB])
        rden = sb("rden", [P, H])
        on = sb("on", [P, D])
        onT = sb("onT", [P, DC, P])
        x1 = sb("x1", [P, 2, D])
        st1 = sb("st1", [P, QT, 6])
        mv1 = sb("mv1", [P, QT, 2])
        ve1 = sb("ve1", [P, QT])
        rs1 = sb("rs1", [P, QT])
        neg1 = sb("neg1", [P, QT])
        shift1 = sb("shift1", [P, QT])
        st2 = sb("st2", [P, 6])
        mv2 = sb("mv2", [P, 2])
        ve2 = sb("ve2", [P, 1])
        rs2 = sb("rs2", [P, 1])
        neg2 = sb("neg2", [P, 1])
        shift2 = sb("shift2", [P, 1])
        rows = sb("rows", [P, 4, TOP_K, RW])
        xn2T = sb("xn2T", [P, DC, P])
        logit = sb("logit", [P, E])
        top = sb("top", [P, 8])
        topi = sb("topi", [P, 8], U32)
        topf = sb("topf", [P, TOP_K])
        chosen = sb("chosen", [P, TOP_K, E])
        chosen_any = sb("chosen_any", [P, E], BF16)
        gap = sb("gap", [P, 1])
        egap = sb("egap", [P, 1])
        wsum = sb("wsum", [P, 1])
        wrec = sb("wrec", [P, 1])
        pos = sb("pos", [P, E])
        base = sb("base", [P, E])
        picked = sb("picked", [P, TOP_K, E])
        slotf = sb("slotf", [P, TOP_K])
        slot = sb("slot", [P, 4, TOP_K], I32)
        base_i = sb("base_i", [P, E], I32)
        cnt_f = sb("cnt_f", [P, E])
        cnt_i = sb("cnt_i", [P, E], I32)
        nt_i = sb("nt_i", [P, E], I32)
        nt_f = sb("nt_f", [P, E])
        one_e = sb("one_e", [P, E])
        tend = sb("tend", [P, E])
        skip = sb("skip", [P, E])
        tile_i = sb("tile_i", [P, MOE_T], I32)
        tile_f = sb("tile_f", [P, MOE_T])
        past = sb("past", [P, MOE_T, E])
        texp = sb("texp", [P, MOE_T])
        texp2 = sb("texp2", [P, MOE_T])
        tblk = sb("tblk", [P, MOE_T])
        raw = sb("raw", [P, 4, DC, D])
        mask_sb = prob[:].rearrange("p t n -> p (t n)").bitcast(I32)[:, 0:B * K2]

        attention.close()
        memory = ctx
        w_all = sb("w_all", [P, NQ, 2, FR, F], F32R)

        banks4 = ps("banks4", [P, 4, 512])
        psS, psK, psY = banks4[:, 0:3], banks4[:, 3], banks4[:, 3, D:2 * D]
        psT = ps("psT", [P, 512])
        psG = ps("psG", [P, 512])
        psA = ps("psA", [P, 512])
        psB = ps("psB", [P, 512])

        raw_in, const_in, mask_in, gates_in = sem("raw_in"), sem("const_in"), sem("mask_in"), sem("gates_in")
        raw_w, w_lo, w_hi, split_out, w_in = sem("raw_w"), sem("w_lo"), sem("w_hi"), sem("split_out"), sem("w_in")
        gate_in, x_in, ctx_in_s = sem("gate_in"), [sem("x_in0"), sem("x_in1")], [sem("ctx_in0"), sem("ctx_in1")]
        x1_out, pad_out, scattered = [sem("x1_out0"), sem("x1_out1")], sem("pad_out"), [sem(f"scattered{j}") for j in range(4)]
        iota_done, ident_done, dv_const = sem("iota_done"), sem("ident_done"), sem("dv_const")
        wT_ps, wT_sb, tanh_done, valid_done = sem("wT_ps"), sem("wT_sb"), sem("tanh_done"), sem("valid_done")
        stat1, mvar1, eps1, rstd1, xn_done = sem("stat1"), sem("mvar1"), sem("eps1"), sem("rstd1"), sem("xn_done")
        xg_done, kbd_done, mrow_done = sem("xg_done"), sem("kbd_done"), sem("mrow_done")
        ctxT_ps, ctxT_sb, xT_ps, xT_sb = sem("ctxT_ps"), sem("ctxT_sb"), sem("xT_ps"), sem("xT_sb")
        k_ps, k_sb, q_ps, q_sb, v_ps, v_sb = (sem(n) for n in ("k_ps", "k_sb", "q_ps", "q_sb", "v_ps", "v_sb"))
        q_lo, k_raw, k_hi = sem("q_lo"), sem("k_raw"), sem("k_hi")
        half_done = sem("half_done")
        neg1_done, neg2_done = sem("neg1_done"), sem("neg2_done")
        v_nat, v_part, v_rest = sem("v_nat"), sem("v_part"), sem("v_rest")
        s_ps, s_max, s_sub, p_done = sem("s_ps"), sem("s_max"), sem("s_sub"), sem("p_done")
        s_neg, s_heads = sem("s_neg"), sem("s_heads")
        t_ps, t_sb, o_ps, o_rec, o_sb = sem("t_ps"), sem("t_sb"), sem("o_ps"), sem("o_rec"), sem("o_sb")
        oT_ps, oT_sb, y_ps, x1_done = sem("oT_ps"), sem("oT_sb"), sem("y_ps"), sem("x1_done")
        stat2, mvar2, eps2, rstd2, xn2_done = sem("stat2"), sem("mvar2"), sem("eps2"), sem("rstd2"), sem("xn2_done")
        n2T_ps, n2T_sb, g_ps, r_ps = sem("n2T_ps"), sem("n2T_sb"), sem("g_ps"), sem("r_ps")
        l_cp, l_max, l_idx, l_idf, l_oh, l_any, gap_done = (
            sem(n) for n in ("l_cp", "l_max", "l_idx", "l_idf", "l_oh", "l_any", "gap_done"))
        egap_done, w_sum, w_rec, w_one, w_done = (sem(n) for n in ("egap_done", "w_sum", "w_rec", "w_one", "w_done"))
        pos_done, base_done, pick_done, slotf_done, slot_done = (
            sem(n) for n in ("pos_done", "base_done", "pick_done", "slotf_done", "slot_done"))
        row_copy, row_id = sem("row_copy"), sem("row_id")
        passed = {e.engine: sem(f"passed{n}") for n, e in enumerate((nc.sync, nc.gpsimd, nc.vector))}
        tab, tab_done = sem("tab"), sem("tab_done")
        et_in, etT_ps, etT_hi, etT_lo, h0_ps, h1_ps = [sem("et_in0"), sem("et_in1")], sem("etT_ps"), sem("etT_hi"), sem("etT_lo"), sem("h0_ps"), sem("h1_ps")
        hs_done, hg_done, hgT_ps, hgT_hi, hgT_lo, ey_ps, ey_done, eid_done, added = (
            sem(n) for n in ("hs_done", "hg_done", "hgT_ps", "hgT_hi", "hgT_lo", "ey_ps", "ey_done", "eid_done", "added"))

        CONST_LOADS = 1 + 3 * 2
        N_IOTA = 8
        UNR = 2
        LOOPS = B // UNR
        PEELED = 2

        def batches(eng, body):
            for b in range(PEELED * UNR):
                body(b, b % UNR, b // UNR)
            with eng.Fori(PEELED, LOOPS - 1) as it:
                for u in range(UNR):
                    body(it * UNR + u, u, it)
            for u in range(UNR):
                body(B - UNR + u, u, LOOPS - 1)

        def tiles(eng, body, n=MOE_T, unroll=4):
            turns = n // unroll
            assert n - turns * unroll >= 2
            for u in range(unroll):
                body(u, u, 0)
            with eng.Fori(1, turns) as it:
                for u in range(unroll):
                    body(it * unroll + u, u, it)
            for u in range(n - turns * unroll):
                body(turns * unroll + u, u, turns)

        def known(v, least):
            return not isinstance(v, int) or v >= least

        def below(v, end):
            return not isinstance(v, int) or v < end

        def after(eng, *waits):
            for done, v in waits:
                eng.wait_ge(done, v)
            if waits:
                eng.sem_inc(passed[eng.engine], 1)

        def pad_experts(eng, experts):
            eng.wait_ge(tab, 1)
            for e in experts:
                r = eng.value_load(base_i[0:1, e:e + 1], min_val=e * REGION * P, max_val=e * REGION * P + NT * P)
                eng.dma_start(routed[bass.ds(r, P), :], pad_rows[:]).then_inc(pad_out, 16)

        block = ctx.enter_context(nc.Block())

        @block.sync
        def _(sp):
            def load_batch(b, u):
                sp.dma_start(xb[:, u], x_t[b] if isinstance(b, int) else x_t[bass.ds(b, 1)].rearrange("o p t d -> p (o t) d")).then_inc(x_in[u], 16)
                sp.dma_start(cb[:, u], ctx_in[b] if isinstance(b, int) else ctx_in[bass.ds(b, 1)].rearrange("o k d -> k (o d)")).then_inc(ctx_in_s[u], 16)

            sp.dma_start(xb[:, 0], x_t[0]).then_inc(x_in[0], 16)
            sp.dma_start(cb[:, 0], ctx_in[0]).then_inc(ctx_in_s[0], 16)
            for n, w in enumerate((Wk, Wq, Wv, Wfc)):
                sp.dma_start(raw[:, n], w.rearrange("(c p) d -> p c d", p=P)).then_inc(raw_in, 16)
            load_batch(1, 1)
            sp.dma_start(gate_sb[:], gate_kernel.rearrange("(c p) e -> p c e", p=P)).then_inc(gate_in, 16)
            sp.wait_ge(dv_const, 1)
            sp.dma_start(out[NT * P:NT * P + P, :], pad_rows[:, 0:D]).then_inc(pad_out, 16)
            sp.wait_ge(dv_const, 2)
            for s in range(SPARE):
                t0 = (E * REGION + s) * P
                sp.dma_start(routed[t0:t0 + P, :], pad_rows[:]).then_inc(pad_out, 16)

            def load_piece(q):
                for n, w in enumerate((w0, w1)):
                    rows_ = w.rearrange("e k f -> (e k) f")
                    sp.dma_start(w_raw[:, n], rows_[bass.ds(q * P, P), :]).then_inc(raw_w, 16)
                rows_ = wo.rearrange("e k d -> (e k) d")
                src = rows_[bass.ds(q * 2 * P, 2 * P), :].rearrange("(o p) d -> p o d", o=2)
                sp.dma_start(w_raw[:, 2].rearrange("p (o d) -> p o d", o=2), src).then_inc(raw_w, 16)

            def store_piece(q):
                sp.wait_ge(w_lo, FR * (q + 1))
                dst = split_w[q] if isinstance(q, int) else split_w[bass.ds(q, 1)].rearrange("o p n -> p (o n)")
                sp.dma_start(dst, w_part[:].rearrange("p s r f -> p (s r f)").bitcast(F32)).then_inc(split_out, 16)

            def fetch_part(q, part):
                if q or part:
                    sp.wait_ge(w_in, 16 * (2 * q + part))
                sp.dma_start(w_all[:, q, part].rearrange("p r f -> p (r f)").bitcast(F32), split_w[q][:, part * QW:(part + 1) * QW]).then_inc(w_in, 16)

            load_piece(0)

            def store_x1(i, slot_):
                sp.wait_ge(x1_done, i + 1)
                dst = out[i * P:(i + 1) * P, :] if isinstance(i, int) else out[bass.ds(i * P, P), :]
                sp.dma_start(dst, x1[:, slot_]).then_inc(x1_out[slot_], 16)

            def batch(b, u, n):
                if below(b, B - 2):
                    after(sp, (xn_done, QT * (b + 1)))
                    after(sp, (xg_done, QT * (b + 1)))
                    after(sp, (ctxT_ps, b + 1))
                    load_batch(b + 2, u)
                if u == 0 and known(n, 1):
                    store_piece(n - 1)
                    load_piece(n)
                early = not below(b, B - UNR)
                if known(b, 1):
                    store_x1(b * QT - 1, 1)
                if early:
                    sp.wait_ge(split_out, 16 * (LOOPS - 1))
                    fetch_part(u * DC, 0)
                    fetch_part(u * DC, 1)
                store_x1(b * QT, 0)
                if early:
                    fetch_part(u * DC + 1, 0)
                    fetch_part(u * DC + 1, 1)

            batches(sp, batch)
            store_piece(NQ - 1)
            store_x1(NT - 1, 1)

            pad_experts(sp, range(0, E, 2))
            sp.wait_ge(pad_out, 16 * (1 + E + SPARE))
            for done in x1_out:
                sp.wait_ge(done, 16 * B)
            for done in (*scattered, tab_done):
                sp.wait_ge(done, 32 * NT // 4 if done is not tab_done else 1)
            for done in et_in:
                sp.wait_ge(done, 16)
            sp.wait_ge(split_out, 16 * NQ)
            for q in range(EARLY, NQ):
                for part in range(2):
                    fetch_part(q, part)

        @block.gpsimd
        def _(gp):
            gp.memset(ident[:], 0.0).then_inc(iota_done, 1)
            gp.wait_ge(iota_done, 1)
            gp.affine_select(out=ident[:], in_=ident[:], compare_op=ALU.not_equal, fill=1.0, base=0,
                             pattern=[[-1, P]], channel_multiplier=1).then_inc(ident_done, 1)
            gp.iota(head_i[:], [[P, CH], [-K2, H]], base=0, channel_multiplier=1).then_inc(iota_done, 1)
            gp.iota(own_i[:], [[-HD, HC]], base=0, channel_multiplier=1).then_inc(iota_done, 1)
            gp.iota(token_i[:], [[P, NT]], base=0, channel_multiplier=1).then_inc(iota_done, 1)
            gp.iota(expert_i[:], [[0, 2], [1, E]], base=0, channel_multiplier=0).then_inc(iota_done, 1)
            gp.iota(tile_i[:], [[1, MOE_T]], base=0, channel_multiplier=0).then_inc(iota_done, 1)
            gp.iota(pad_i[:], [[0, 1]], base=NT * P, channel_multiplier=1).then_inc(iota_done, 1)
            gp.memset(upper[:], 1.0).then_inc(iota_done, 1)
            gp.wait_ge(iota_done, N_IOTA)
            gp.affine_select(out=upper[:], in_=upper[:], compare_op=ALU.is_gt, fill=0.0, base=0,
                             pattern=[[1, P]], channel_multiplier=-1).then_inc(ident_done, 1)

            def rstd_1(b):
                after(gp, (mvar1, QT * (b + 1)))
                gp.tensor_scalar(ve1[:], mv1[:, :, 1], EPS, 1.0, ALU.add, ALU.mult).then_inc(eps1, 1)
                gp.tensor_scalar(neg1[:], mv1[:, :, 0], 0.0, -1.0, ALU.add, ALU.mult).then_inc(eps1, 1)
                if known(b, 1):
                    gp.wait_ge(xn_done, QT * b)
                gp.wait_ge(eps1, 2 * (b + 1))
                gp.tensor_tensor(rs1[:], ve1[:], half_neg[:], ALU.pow).then_inc(neg1_done, 1)
                gp.wait_ge(neg1_done, b + 1)
                gp.tensor_tensor(shift1[:], neg1[:], rs1[:], ALU.mult).then_inc(rstd1, 1)

            def spread_keys(b, u):
                after(gp, *([(s_ps, QT * (b - 1))] if known(b, 2) else []))
                gp.tensor_copy(mrow[:, u], masked[:, bass.ds(b * K2, K2)]).then_inc(mrow_done, 1)
                gp.wait_ge(k_sb, b + 1)
                for a, c in ((a, c) for a in range(2) for c in range(DC)):
                    gp.tensor_tensor(kbd[:, u, a, c], kT2[:, a, c].bitcast(F32).rearrange("p (o k) -> p o k", o=1).to_broadcast([P, HC, K2]),
                                     own[:].rearrange("p (h o) -> p h o", o=1).to_broadcast([P, HC, K2]), ALU.mult).then_inc(kbd_done, 1)

            def residual(b, u, n):
                gp.wait_ge(x_in[u], 16 * (n + 1))
                if known(b, 2):
                    gp.wait_ge(x1_done, QT * (b - 1))
                for t in range(QT):
                    gp.tensor_tensor(xg[:, u, t], xb[:, u, t], bfc_rows[:], ALU.add).then_inc(xg_done, 1)

            gp.wait_ge(half_done, 1)
            rstd_1(0)
            rstd_1(1)
            gp.wait_ge(dv_const, 2)
            spread_keys(0, 0)
            residual(0, 0, 0)

            def rstd_2(i):
                after(gp, (mvar2, i + 1))
                gp.tensor_scalar(ve2[:], mv2[:, 1:2], EPS, 1.0, ALU.add, ALU.mult).then_inc(eps2, 1)
                gp.tensor_scalar(neg2[:], mv2[:, 0:1], 0.0, -1.0, ALU.add, ALU.mult).then_inc(eps2, 1)
                if known(i, 1):
                    gp.wait_ge(xn2_done, i)
                gp.wait_ge(eps2, 2 * (i + 1))
                gp.tensor_tensor(rs2[:], ve2[:], half_neg[:, 0:1], ALU.pow).then_inc(neg2_done, 1)
                gp.wait_ge(neg2_done, i + 1)
                gp.tensor_tensor(shift2[:], neg2[:], rs2[:], ALU.mult).then_inc(rstd2, 1)

            def number_rows(i, u4):
                after(gp, (xn2_done, i + 1))
                gp.tensor_copy(rows[:, u4, :, D], token_id[:, bass.ds(i, 1)].to_broadcast([P, TOP_K])).then_inc(row_id, 1)

            def weigh(i, u4):
                after(gp, (egap_done, i + 1))
                gp.tensor_scalar(wsum[:], egap[:], 1.0, 1.0, ALU.add, ALU.mult).then_inc(w_sum, 1)
                gp.wait_ge(w_sum, i + 1)
                gp.tensor_tensor(wrec[:], wsum[:], neg_one[:], ALU.pow).then_inc(w_rec, 1)
                gp.wait_ge(w_rec, i + 1)
                gp.tensor_tensor(rows[:, u4, 0, D + 1:D + 2], wrec[:], tanhg[:, 1:2], ALU.mult).then_inc(w_one, 1)
                gp.wait_ge(w_one, i + 1)
                gp.tensor_tensor(rows[:, u4, 1, D + 1:D + 2], rows[:, u4, 0, D + 1:D + 2], egap[:], ALU.mult).then_inc(w_done, 1)

            def scatter(i, u4):
                after(gp, (slot_done, i + 1), (w_done, i + 1), (row_copy, i + 1), (row_id, i + 1))
                for k in range(TOP_K):
                    gp.indirect_dma_start(out=routed, out_offset=bass.IndirectOffsetOnAxis(ap=slot[:, u4, k:k + 1], axis=0),
                                          in_=rows[:, u4, k, :], in_offset=None).then_inc(scattered[u4], 16)

            def split_low(q, r):
                after(gp, (w_hi, FR * q + r + 1))
                gp.tensor_tensor(w_part[:, 1, r], w_raw[:, r], w_part[:, 0, r].bitcast(F32), ALU.subtract).then_inc(w_lo, 1)

            def batch(b, u, n):
                more, more2 = below(b, B - 1), below(b, B - 2)
                for t in range(QT):
                    i = b * QT + t
                    u4 = u * QT + t
                    if t == 0 and more:
                        spread_keys(b + 1, 1 - u)
                    if known(i, 4):
                        scatter(i - 4, u4)
                    if t == 0 and known(i, 1):
                        rstd_2(i - 1)
                    if t == 1 and more:
                        residual(b + 1, 1 - u, n + u)
                    if t == 0 and more2:
                        rstd_1(b + 2)
                    if known(i, 2):
                        number_rows(i - 2, (u4 - 2) % 4)
                    if known(i, 3):
                        weigh(i - 3, (u4 - 3) % 4)
                    if t == 1:
                        rstd_2(i - 1)
                    if u4 >= 4 - FR:
                        split_low(n, u4 - (4 - FR))

            batches(gp, batch)
            weigh(NT - 3, 1)
            number_rows(NT - 2, 2)
            scatter(NT - 4, 0)
            rstd_2(NT - 1)
            scatter(NT - 3, 1)
            weigh(NT - 2, 2)
            scatter(NT - 2, 2)
            number_rows(NT - 1, 3)
            weigh(NT - 1, 3)
            scatter(NT - 1, 3)

            def load_rows(t, u):
                if known(t, 2):
                    after(gp, (etT_ps, t - 1), (eid_done, 2 * (t - 1)))
                r = gp.value_load(tblk_i[0:1, bass.ds(t, 1)], min_val=0, max_val=E * REGION + SPARE - 1)
                gp.dma_start(et[:, u % 2], routed[bass.ds(r * P, P), :]).then_inc(et_in[u % 2], 16)

            def add_rows(t, u):
                after(gp, (ey_done, t + 1), (eid_done, 2 * (t + 1)), *([(added, 16 * t)] if known(t, 1) else []))
                gp.indirect_dma_start(out=out, out_offset=bass.IndirectOffsetOnAxis(ap=eid[:, u:u + 1], axis=0),
                                      in_=ey[:, u % 2, :], in_offset=None, compute_op=ALU.add).then_inc(added, 16)

            gp.wait_ge(tab_done, 1)
            for done in x1_out:
                gp.wait_ge(done, 16 * B)
            gp.wait_ge(pad_out, 16 * (1 + E + SPARE))
            for done in scattered:
                gp.wait_ge(done, 32 * NT // 4)
            load_rows(0, 0)
            load_rows(1, 1)

            def tile(t, u, q):
                if known(t, 2):
                    add_rows(t - 2, (u - 2) % 4)
                if below(t, MOE_T - 2):
                    load_rows(t + 2, u + 2)

            tiles(gp, tile)
            for t in range(MOE_T - 2, MOE_T):
                add_rows(t, t % 4)
            gp.wait_ge(added, 16 * MOE_T)

        @block.scalar
        def _(act):
            act.dma_start(mask_sb, mask.rearrange("b k -> (b k)").rearrange("(o n) -> o n", o=1).to_broadcast([P, B * K2])).then_inc(mask_in, 16)
            act.dma_start(gates[:, 0:1], gx.to_broadcast([P, 1])).then_inc(gates_in, 16)
            act.dma_start(gates[:, 1:2], gf.to_broadcast([P, 1])).then_inc(gates_in, 16)
            act.dma_start(bfc_rows[:], bfc.rearrange("(o d) -> o d", o=1).to_broadcast([P, D])).then_inc(const_in, 16)
            with nc.allow_non_contiguous_dma(reason="biases, one word a partition"):
                for n, v in enumerate((bq, bk, bv)):
                    for a in range(DC):
                        act.dma_start(bias[:, n, a:a + 1], v[a * P:(a + 1) * P].rearrange("(q o) -> q o", o=1)).then_inc(const_in, 16)
            act.wait_ge(gates_in, 32)
            act.activation(tanhg[:], gates[:], ACT.Tanh).then_inc(tanh_done, 1)
            for n, name in enumerate(wT):
                act.wait_ge(wT_ps, n + 1)
                act.copy(wT[name][:].rearrange("p c d -> p (c d)"), banks4[:, n]).then_inc(wT_sb, 1)
            act.wait_ge(const_in, 16 * CONST_LOADS)

            def ctx_evac(b):
                act.wait_ge(ctxT_ps, b + 1)
                if known(b, 1):
                    act.wait_ge(v_nat, b)
                act.copy(ctxT[:].rearrange("p c k -> p (c k)"), psK[:, 0:DC * K2]).then_inc(ctxT_sb, 1)

            def norm_1(b, u):
                act.wait_ge(rstd1, b + 1)
                if known(b, 1):
                    act.wait_ge(xT_ps, b)
                for t in range(QT):
                    act.activation(xn[:, t], xb[:, u, t], ACT.Identity, bias=shift1[:, t:t + 1], scale=rs1[:, t:t + 1]).then_inc(xn_done, 1)

            def x_evac(b):
                act.wait_ge(xT_ps, b + 1)
                act.copy(xnT[:].rearrange("p c s -> p (c s)"), psA[:]).then_inc(xT_sb, 1)

            def q_evac(b, u):
                act.wait_ge(q_ps, b + 1)
                for a in range(DC):
                    act.activation(qT[:, u, 0, a], psA[:, a * S:(a + 1) * S], ACT.Identity, bias=bias[:, 0, a:a + 1]).then_inc(q_sb, 1)

            def t_evac(i, g):
                c0, c1 = T_GROUPS[g]
                act.wait_ge(t_ps, 3 * i + g + 1)
                if known(i, 1) and g == 0:
                    act.wait_ge(o_ps, i)
                act.copy(probT[:, c0:c1].rearrange("p c q -> p (c q)"), psT[:, 0:(c1 - c0) * P]).then_inc(t_sb, 1)

            def exp_scores(i, t):
                act.wait_ge(s_neg, i + 1)
                for j, h in enumerate(range(S_FULL * HB, H)):
                    act.activation(prob[:, t, h * K2:(h + 1) * K2], psS[:, S_FULL, j * K2:(j + 1) * K2], ACT.Exp,
                                   bias=neg_mx[:, t, j:j + 1], scale=scale).then_inc(s_heads, 1)
                act.wait_ge(s_sub, i + 1)
                shifted = prob[:, t, 0:S_FULL * HB * K2]
                act.activation(shifted, shifted, ACT.Exp, scale=scale).then_inc(p_done, 1)

            def norm_2(i, t, u4, n):
                act.wait_ge(rstd2, i + 1)
                if known(n, 1):
                    act.wait_ge(scattered[u4], 32 * n)
                act.activation(rows[:, u4, 0, 0:D], x1[:, t], ACT.Identity, bias=shift2[:], scale=rs2[:]).then_inc(xn2_done, 1)

            def n2_evac(i):
                act.wait_ge(n2T_ps, i + 1)
                act.copy(xn2T[:].rearrange("p c q -> p (c q)"), psG[:, 0:D]).then_inc(n2T_sb, 1)

            def l_evac(i):
                act.wait_ge(g_ps, i + 1)
                if known(i, 1):
                    act.wait_ge(l_idx, i)
                act.copy(logit[:], psG[:, D:D + E]).then_inc(l_cp, 1)

            def exp_gap(i):
                act.wait_ge(gap_done, i + 1)
                if known(i, 1):
                    act.wait_ge(w_done, i)
                act.activation(egap[:], gap[:], ACT.Exp).then_inc(egap_done, 1)

            def o_evac(i):
                act.wait_ge(oT_ps, i + 1)
                for c in range(DC):
                    act.activation(onT[:, c], psY[:, c * P:(c + 1) * P], ACT.Identity, bias=bias[:, 2, c:c + 1]).then_inc(oT_sb, 1)

            def split_high(q, r):
                act.wait_ge(raw_w, 16 * 3 * (q + 1))
                if known(q, 1):
                    act.wait_ge(split_out, 16 * q)
                act.copy(w_part[:, 0, r], w_raw[:, r]).then_inc(w_hi, 1)

            def copy_row(i, u4):
                act.wait_ge(xn2_done, i + 1)
                act.copy(rows[:, u4, 1, 0:D], rows[:, u4, 0, 0:D]).then_inc(row_copy, 1)

            def v_first(b):
                act.wait_ge(v_nat, b + 1)
                act.copy(vparts[:, 0], psA[0:K2, 0:D]).then_inc(v_part, 1)

            norm_1(0, 0)
            ctx_evac(0)
            x_evac(0)
            norm_1(1, 1)
            q_evac(0, 0)
            v_first(0)
            ctx_evac(1)
            exp_scores(0, 0)
            x_evac(1)
            t_evac(0, 0)

            def batch(b, u, n):
                more, more2 = below(b, B - 1), below(b, B - 2)
                for t in range(QT):
                    i = b * QT + t
                    u4 = u * QT + t
                    t_evac(i, 1)
                    if known(i, 1):
                        o_evac(i - 1)
                    if known(i, 2):
                        norm_2(i - 2, t, (u4 - 2) % 4, n if u4 >= 2 else n - 1)
                    if t == 0 and more:
                        q_evac(b + 1, 1 - u)
                    t_evac(i, 2)
                    if t == 1 and more2:
                        norm_1(b + 2, u)
                    if known(i, 3):
                        exp_gap(i - 3)
                    if known(i, 2):
                        n2_evac(i - 2)
                    if t == 0 or more:
                        exp_scores(i + 1, 1 - t)
                    if known(i, 2):
                        copy_row(i - 2, (u4 - 2) % 4)
                        l_evac(i - 2)
                    if u4 >= 4 - FR:
                        split_high(n, u4 - (4 - FR))
                    if t == 1 and more2:
                        x_evac(b + 2)
                    if t == 0 and more:
                        v_first(b + 1)
                    if t == 0 or more:
                        t_evac(i + 1, 0)
                    if t == 0 and more2:
                        ctx_evac(b + 2)

            batches(act, batch)
            o_evac(NT - 1)
            exp_gap(NT - 3)
            norm_2(NT - 2, 0, 2, LOOPS - 1)
            n2_evac(NT - 2)
            copy_row(NT - 2, 2)
            l_evac(NT - 2)
            exp_gap(NT - 2)
            norm_2(NT - 1, 1, 3, LOOPS - 1)
            n2_evac(NT - 1)
            copy_row(NT - 1, 3)
            l_evac(NT - 1)
            exp_gap(NT - 1)
            pad_experts(act, range(1, E, 2))

            def e_evac(t, u):
                act.wait_ge(etT_ps, t + 1)
                act.copy(etT[:, u % 2, 0].rearrange("p c q -> p (c q)"), psG[:, 0:D]).then_inc(etT_hi, 1)

            def silu(t, u):
                act.wait_ge(h0_ps, t + 1)
                if known(t, 1):
                    act.wait_ge(hgT_ps, t)
                act.activation(hs[:], banks4[:, u % 2], ACT.Silu).then_inc(hs_done, 1)

            def g_evac(t):
                act.wait_ge(hgT_ps, t + 1)
                if known(t, 1):
                    act.wait_ge(ey_ps, t)
                act.copy(hgT[:, 0].rearrange("p c q -> p (c q)"), psT[:]).then_inc(hgT_hi, 1)

            def y_evac(t, u):
                act.wait_ge(ey_ps, t + 1)
                if known(t, 2):
                    act.wait_ge(added, 16 * (t - 1))
                act.activation(ey[:, u % 2], psB[:, 0:D], ACT.Copy, scale=ewt[:, u:u + 1]).then_inc(ey_done, 1)

            e_evac(0, 0)

            def tile(t, u, q):
                silu(t, u)
                if known(t, 1):
                    g_evac(t - 1)
                if below(t, MOE_T - 1):
                    e_evac(t + 1, u + 1)
                if known(t, 1):
                    y_evac(t - 1, (u - 1) % 4)

            tiles(act, tile)
            g_evac(MOE_T - 1)
            y_evac(MOE_T - 1, (MOE_T - 1) % 4)

        @block.vector
        def _(dve):
            dve.memset(half_neg[:], -0.5).then_inc(half_done, 1)
            dve.memset(pad_rows[:, 0:D], 0.0).then_inc(dv_const, 1)
            dve.memset(pad_rows[:, D + 1:D + 2], 0.0).then_inc(valid_done, 1)
            dve.memset(neg_one[:], -1.0).then_inc(valid_done, 1)
            dve.memset(ones[:], 1.0).then_inc(valid_done, 1)
            dve.memset(share[:], 1.0 / P).then_inc(valid_done, 1)
            dve.memset(one_e[:], 1.0).then_inc(valid_done, 1)
            def stats_1(b, u, n):
                dve.wait_ge(x_in[u], 16 * (n + 1))
                if known(b, 1):
                    dve.wait_ge(rstd1, b)
                for t in range(QT):
                    dve.bn_stats(st1[:, t], xb[:, u, t]).then_inc(stat1, 1)
                after(dve, (stat1, QT * (b + 1)))
                for t in range(QT):
                    dve.bn_aggr(mv1[:, t], st1[:, t]).then_inc(mvar1, 1)

            stats_1(0, 0, 0)
            stats_1(1, 1, 0)
            dve.wait_ge(iota_done, N_IOTA)
            dve.tensor_copy(pad_rows[:, D:D + 1], pad_i[:]).then_inc(valid_done, 1)
            dve.tensor_copy(token_id[:], token_i[:]).then_inc(valid_done, 1)
            dve.tensor_copy(expert_f[:], expert_i[:]).then_inc(valid_done, 1)
            dve.tensor_copy(tile_f[:], tile_i[:]).then_inc(valid_done, 1)
            dve.tensor_copy(head_f[:], head_i[:]).then_inc(valid_done, 1)
            dve.tensor_copy(own_f[:], own_i[:]).then_inc(valid_done, 1)
            dve.wait_ge(valid_done, 11)
            dve.tensor_scalar(head_lt[:], head_f[:], K2 - 0.5, None, ALU.is_lt).then_inc(valid_done, 1)
            dve.tensor_scalar(own_lt[:], own_f[:], HD - 0.5, None, ALU.is_lt).then_inc(valid_done, 1)
            dve.tensor_scalar(region0[:], expert_f[:, 0], float(REGION * P), None, ALU.mult).then_inc(valid_done, 1)
            dve.tensor_scalar(base[:], expert_f[:, 0], float(REGION * P), None, ALU.mult).then_inc(valid_done, 1)
            dve.wait_ge(valid_done, 15)
            dve.scalar_tensor_tensor(out=own[:], in0=own_f[:], scalar=-0.5, in1=own_lt[:], op0=ALU.is_gt, op1=ALU.mult).then_inc(valid_done, 1)
            dve.scalar_tensor_tensor(out=head_f[:], in0=head_f[:], scalar=-0.5, in1=head_lt[:], op0=ALU.is_gt, op1=ALU.mult).then_inc(valid_done, 1)
            dve.wait_ge(valid_done, 17)
            for c in range(CH):
                dve.tensor_copy(head_of[:, c], head_f[:, c, first_head[c]:first_head[c] + 3]).then_inc(valid_done, 1)
            dve.wait_ge(valid_done, 17 + CH)
            for u in range(2):
                dve.tensor_copy(vbd[:, u, :, :, HD], head_of[:]).then_inc(valid_done, 1)
            dve.wait_ge(mask_in, 16)
            dve.tensor_scalar(valid[:], mask_sb, 0, None, ALU.not_equal).then_inc(valid_done, 1)
            dve.tensor_scalar(masked[:], mask_sb, 0, MASKED / scale, ALU.is_equal, ALU.mult).then_inc(valid_done, 1)
            dve.wait_ge(const_in, 16 * CONST_LOADS)
            dve.wait_ge(tanh_done, 1)
            dve.tensor_scalar(bfc_rows[:], bfc_rows[:], tanhg[:, 0:1], None, ALU.mult).then_inc(valid_done, 1)
            dve.wait_ge(valid_done, 22 + CH)
            dve.memset(prob[:, :, HK:CH * P], 0.0).then_inc(valid_done, 1)
            dve.wait_ge(ident_done, 2)
            dve.tensor_copy(pick_key[:].rearrange("p (o k) -> p o k", o=3), ident[0:K2, 0:K2].rearrange("p (o k) -> p o k", o=1).to_broadcast([K2, 3, K2])).then_inc(valid_done, 1)
            dve.wait_ge(valid_done, 24 + CH)
            dve.engine_nop().then_inc(dv_const, 1)

            def biased_low(dst, ps_part, bias_part, high):
                return dve.scalar_tensor_tensor(out=dst, in0=ps_part, scalar=bias_part, in1=high.bitcast(F32), op0=ALU.add, op1=ALU.subtract)

            def q_low(b, u):
                dve.wait_ge(q_sb, DC * (b + 1))
                for a in range(DC):
                    biased_low(qT[:, u, 1, a], psA[:, a * S:(a + 1) * S], bias[:, 0, a:a + 1], qT[:, u, 0, a]).then_inc(q_lo, 1)

            def k_evac(b):
                dve.wait_ge(k_ps, b + 1)
                if known(b, 1):
                    dve.wait_ge(kbd_done, 2 * DC * b)
                for a in range(DC):
                    dve.scalar_tensor_tensor(out=kT[:, a], in0=psK[:, a * K2:(a + 1) * K2], scalar=bias[:, 1, a:a + 1],
                                             in1=valid[:, bass.ds(b * K2, K2)], op0=ALU.add, op1=ALU.mult).then_inc(k_raw, 1)

            def k_split(b, part):
                dve.wait_ge(k_raw, DC * (b + 1))
                if part == 0:
                    dve.tensor_copy(kT2[:, 0], kT[:]).then_inc(k_hi, 1)
                else:
                    dve.wait_ge(k_hi, b + 1)
                    dve.tensor_tensor(kT2[:, 1], kT[:], kT2[:, 0].bitcast(F32), ALU.subtract).then_inc(k_sb, 1)

            def v_split(b, part):
                if part == 0:
                    dve.wait_ge(v_part, 3 * b + 1)
                    dve.tensor_tensor(vrest[:], psA[0:K2, 0:D], vparts[:, 0], ALU.subtract).then_inc(v_rest, 1)
                elif part == 1:
                    dve.wait_ge(v_rest, b + 1)
                    dve.tensor_copy(vparts[:, 1], vrest[:]).then_inc(v_part, 1)
                else:
                    dve.wait_ge(v_part, 3 * b + 2)
                    dve.tensor_tensor(vparts[:, 2], vrest[:], vparts[:, 1], ALU.subtract).then_inc(v_part, 1)

            def v_evac(b, u):
                dve.wait_ge(v_ps, b + 1)
                dve.tensor_tensor(vbd[:, u, :, :, 0:HD].rearrange("p c h d -> p (c h) d"),
                                  psA[:, 0:CH * 3 * HD].rearrange("p (n d) -> p n d", d=HD),
                                  head_of[:].rearrange("p c (h o) -> p (c h) o", o=1).to_broadcast([P, CH * 3, HD]), ALU.mult).then_inc(v_sb, 1)

            split = S_FULL * HB
            S_PARTS = [(psS[:, 0:S_FULL, 0:HB * K2].rearrange("p n (h k) -> p n h k", k=K2), 0, S_FULL, HB),
                       (psS[:, S_FULL:S_FULL + 1, 0:(H - split) * K2].rearrange("p n (h k) -> p n h k", k=K2), split, 1, H - split)]

            def s_largest(i, t, part):
                dve.wait_ge(s_ps, i + 1)
                sv, h0, n, k = S_PARTS[part]
                dve.tensor_reduce(mx[:, t, h0:h0 + n * k].rearrange("p (n h) -> p n h", n=n), sv, AX_X, ALU.max).then_inc(s_max, 1)

            def s_negate(i, t):
                dve.wait_ge(s_max, 2 * (i + 1))
                dve.tensor_scalar(neg_mx[:, t], mx[:, t, S_FULL * HB:H], -scale, None, ALU.mult).then_inc(s_neg, 1)

            def s_shift(i, t):
                sv, h0, n, k = S_PARTS[0]
                dve.tensor_tensor(prob[:, t, h0 * K2:(h0 + n * k) * K2].rearrange("p (n h k) -> p n h k", n=n, k=K2), sv,
                                  mx[:, t, h0:h0 + n * k].rearrange("p (n h o) -> p n h o", n=n, o=1).to_broadcast([P, n, k, K2]),
                                  ALU.subtract).then_inc(s_sub, 1)

            def o_norm(i):
                dve.wait_ge(o_ps, i + 1)
                ov = psB[:, 0:H * VW].rearrange("p (h d) -> p h d", d=VW)
                dve.reciprocal(rden[:], ov[:, :, HD]).then_inc(o_rec, 1)
                dve.wait_ge(o_rec, i + 1)
                dve.tensor_tensor(on[:].rearrange("p (h d) -> p h d", d=HD), ov[:, :, 0:HD],
                                  rden[:].rearrange("p (h o) -> p h o", o=1).to_broadcast([P, H, HD]), ALU.mult).then_inc(o_sb, 1)

            def residual_1(i, u, t, b):
                dve.wait_ge(y_ps, i + 1)
                dve.wait_ge(xg_done, QT * (b + 1))
                if known(b, 1):
                    dve.wait_ge(x1_out[t], 16 * b)
                if known(i, 2):
                    dve.wait_ge(xn2_done, i - 1)
                dve.scalar_tensor_tensor(out=x1[:, t], in0=psY, scalar=tanhg[:, 0:1], in1=xg[:, u, t], op0=ALU.mult, op1=ALU.add).then_inc(x1_done, 1)
                dve.wait_ge(x1_done, i + 1)
                dve.bn_stats(st2[:], x1[:, t]).then_inc(stat2, 1)
                after(dve, (stat2, i + 1), *([(rstd2, i)] if known(i, 1) else []))
                dve.bn_aggr(mv2[:], st2[:]).then_inc(mvar2, 1)

            def choose(i):
                after(dve, (l_cp, i + 1))
                dve.max(top[:], logit[:]).then_inc(l_max, 1)
                after(dve, (l_max, i + 1))
                dve.max_index(topi[:], top[:], logit[:]).then_inc(l_idx, 1)
                if known(i, 1):
                    dve.wait_ge(egap_done, i)
                dve.tensor_tensor(gap[:], top[:, 1:2], top[:, 0:1], ALU.subtract).then_inc(gap_done, 1)
                dve.wait_ge(l_idx, i + 1)
                dve.tensor_copy(topf[:], topi[:, 0:TOP_K]).then_inc(l_idf, 1)
                dve.wait_ge(l_idf, i + 1)
                dve.tensor_tensor(chosen[:], expert_f[:], topf[:].rearrange("p (k o) -> p k o", o=1).to_broadcast([P, TOP_K, E]), ALU.is_equal).then_inc(l_oh, 1)
                dve.wait_ge(l_oh, i + 1)
                dve.tensor_tensor(chosen_any[:], chosen[:, 0], chosen[:, 1], ALU.add).then_inc(l_any, 1)

            def free_rows(i, part):
                if part == 0:
                    dve.wait_ge(r_ps, i + 1)
                    dve.tensor_tensor(pos[:], psG[:, D + E:D + 2 * E], base[:], ALU.add).then_inc(pos_done, 1)
                else:
                    dve.wait_ge(pos_done, i + 1)
                    dve.tensor_tensor(base[:], psG[:, D + 2 * E:D + 3 * E], base[:], ALU.add).then_inc(base_done, 1)

            def place(i, u4):
                dve.tensor_tensor(picked[:], chosen[:], pos[:].rearrange("p (o e) -> p o e", o=1).to_broadcast([P, TOP_K, E]), ALU.mult).then_inc(pick_done, 1)
                dve.wait_ge(pick_done, i + 1)
                dve.tensor_reduce(slotf[:], picked[:], AX_X, ALU.add).then_inc(slotf_done, 1)
                dve.wait_ge(slotf_done, i + 1)
                dve.tensor_copy(slot[:, u4], slotf[:]).then_inc(slot_done, 1)
                dve.wait_ge(base_done, i + 1)

            k_evac(0)
            k_split(0, 0)
            k_split(0, 1)
            q_low(0, 0)
            for part in range(3):
                v_split(0, part)
            v_evac(0, 0)
            for part in range(2):
                s_largest(0, 0, part)
            s_negate(0, 0)
            s_shift(0, 0)
            k_evac(1)
            k_split(1, 0)
            k_split(1, 1)

            def batch(b, u, n):
                more, more2 = below(b, B - 1), below(b, B - 2)
                for t in range(QT):
                    i = b * QT + t
                    u4 = u * QT + t
                    keys = t == 0 and known(b, 1) and more
                    softmax = t == 0 or more
                    placed = known(i, 3)
                    if keys:
                        k_evac(b + 1)
                    if t == 1 and more:
                        v_split(b + 1, 0)
                    if softmax:
                        s_largest(i + 1, 1 - t, 0)
                    if keys:
                        k_split(b + 1, 0)
                    if placed:
                        free_rows(i - 3, 0)
                    if softmax:
                        s_largest(i + 1, 1 - t, 1)
                    if keys:
                        k_split(b + 1, 1)
                    if placed:
                        free_rows(i - 3, 1)
                    if t == 1 and more:
                        v_split(b + 1, 1)
                    if softmax:
                        s_negate(i + 1, 1 - t)
                    if t == 1 and more:
                        v_split(b + 1, 2)
                    if softmax:
                        s_shift(i + 1, 1 - t)
                    if t == 0 and more:
                        q_low(b + 1, 1 - u)
                    if t == 0 and more2:
                        stats_1(b + 2, u, n + 1)
                    o_norm(i)
                    if t == 1 and more:
                        v_evac(b + 1, 1 - u)
                    if known(i, 1):
                        residual_1(i - 1, u if t else 1 - u, 1 - t, b if t else b - 1)
                    if known(i, 3):
                        place(i - 3, (u4 - 3) % 4)
                    if known(i, 2):
                        choose(i - 2)

            batches(dve, batch)
            free_rows(NT - 3, 0)
            free_rows(NT - 3, 1)
            residual_1(NT - 1, 1, 1, B - 1)
            place(NT - 3, 1)
            choose(NT - 2)
            free_rows(NT - 2, 0)
            free_rows(NT - 2, 1)
            place(NT - 2, 2)
            choose(NT - 1)
            free_rows(NT - 1, 0)
            free_rows(NT - 1, 1)
            place(NT - 1, 3)

            steps = [0]

            def step(m):
                m.then_inc(tab, 1)
                steps[0] += 1
                dve.wait_ge(tab, steps[0])

            step(dve.tensor_copy(base_i[:], base[:]))
            step(dve.tensor_tensor(cnt_f[:], base[:], region0[:], ALU.subtract))
            step(dve.tensor_scalar(cnt_f[:], cnt_f[:], float(P - 1), None, ALU.add))
            step(dve.tensor_copy(cnt_i[:], cnt_f[:]))
            step(dve.tensor_scalar(nt_i[:], cnt_i[:], P.bit_length() - 1, None, ALU.logical_shift_right))
            step(dve.tensor_copy(nt_f[:], nt_i[:]))
            step(dve.tensor_tensor_scan(tend[:], one_e[:], nt_f[:], 0.0, ALU.mult, ALU.add))
            step(dve.tensor_scalar(skip[:], nt_f[:], -1.0, float(REGION), ALU.mult, ALU.add))
            step(dve.tensor_tensor(past[:], tile_f[:].rearrange("p (t o) -> p t o", o=1).to_broadcast([P, MOE_T, E]),
                                   tend[:].rearrange("p (o e) -> p o e", o=1).to_broadcast([P, MOE_T, E]), ALU.is_ge))
            step(dve.tensor_reduce(texp[:], past[:], AX_X, ALU.add))
            step(dve.tensor_scalar(texp2[:], texp[:], float(E - 1), None, ALU.min))
            step(dve.tensor_copy(texp_i[:], texp2[:]))
            step(dve.tensor_tensor(past[:], past[:], skip[:].rearrange("p (o e) -> p o e", o=1).to_broadcast([P, MOE_T, E]), ALU.mult))
            step(dve.tensor_reduce(tblk[:], past[:], AX_X, ALU.add))
            step(dve.tensor_tensor(tblk[:], tblk[:], tile_f[:], ALU.add))
            step(dve.tensor_copy(tblk_i[:], tblk[:]))
            dve.engine_nop().then_inc(tab_done, 1)

            def glu(t, u):
                dve.wait_ge(h1_ps, t + 1)
                dve.wait_ge(hs_done, t + 1)
                dve.tensor_tensor(hs[:], banks4[:, 2 + u % 2], hs[:], ALU.mult).then_inc(hg_done, 1)

            def g_low(t):
                dve.wait_ge(hgT_hi, t + 1)
                dve.tensor_tensor(hgT[:, 1].rearrange("p c q -> p (c q)"), psT[:], hgT[:, 0].rearrange("p c q -> p (c q)").bitcast(F32),
                                  ALU.subtract).then_inc(hgT_lo, 1)

            def e_low(t, u):
                dve.wait_ge(etT_hi, t + 1)
                dve.tensor_tensor(etT[:, u % 2, 1].rearrange("p c q -> p (c q)"), psG[:, 0:D],
                                  etT[:, u % 2, 0].rearrange("p c q -> p (c q)").bitcast(F32), ALU.subtract).then_inc(etT_lo, 1)
                if known(t, 4):
                    dve.wait_ge(added, 16 * (t - 3))
                dve.tensor_copy(eid[:, u:u + 1], et[:, u % 2, D:D + 1]).then_inc(eid_done, 1)
                dve.tensor_copy(ewt[:, u:u + 1], et[:, u % 2, D + 1:D + 2]).then_inc(eid_done, 1)

            e_low(0, 0)

            def tile(t, u, q):
                if known(t, 1):
                    g_low(t - 1)
                if below(t, MOE_T - 1):
                    e_low(t + 1, (u + 1) % 4)
                glu(t, u)

            tiles(dve, tile)
            g_low(MOE_T - 1)

        @block.tensor
        def _(pe):
            pe.wait_ge(ident_done, 2)
            pe.wait_ge(raw_in, 16 * 4)
            for n in range(4):
                for c in range(DC):
                    for o in range(DC):
                        m = pe.transpose(banks4[:, n, (c * DC + o) * P:(c * DC + o + 1) * P], raw[:, n, o, c * P:(c + 1) * P], ident[:])
                m.then_inc(wT_ps, 1)

            PARTS = ((0, 0), (0, 1), (1, 0))

            def ctx_T(b, u, n):
                pe.wait_ge(ctx_in_s[u], 16 * (n + 1))
                if known(b, 1):
                    pe.wait_ge(k_raw, DC * b)
                for c in range(DC):
                    m = pe.transpose(psK[:, c * K2:(c + 1) * K2], cb[:, u, c * P:(c + 1) * P], ident[0:K2, 0:K2])
                m.then_inc(ctxT_ps, 1)

            def keys(b):
                pe.wait_ge(ctxT_sb, b + 1)
                for a in range(2):
                    for c in range(DC):
                        m = pe.matmul(psK[:, a * K2:(a + 1) * K2], wT["wk"][:, c, a * P:(a + 1) * P], ctxT[:, c], start=(c == 0), stop=(c == DC - 1))
                m.then_inc(k_ps, 1)

            def x_T(b):
                pe.wait_ge(xn_done, QT * (b + 1))
                if known(b, 1):
                    pe.wait_ge(v_sb, b)
                for c in range(DC):
                    for t in range(QT):
                        m = pe.transpose(psA[:, c * S + t * P:c * S + (t + 1) * P], xn[:, t, c * P:(c + 1) * P], ident[:])
                m.then_inc(xT_ps, 1)

            def queries(b, a):
                pe.wait_ge(xT_sb, b + 1)
                for c in range(DC):
                    m = pe.matmul(psA[:, a * S:(a + 1) * S], wT["wq"][:, c, a * P:(a + 1) * P], xnT[:, c], start=(c == 0), stop=(c == DC - 1))
                if a == DC - 1:
                    m.then_inc(q_ps, 1)

            def values(b):
                pe.wait_ge(q_lo, DC * (b + 1))
                for c in range(DC):
                    m = pe.matmul(psA[0:K2, 0:D], ctxT[:, c], wT["wv"][:, c], start=(c == 0), stop=(c == DC - 1))
                m.then_inc(v_nat, 1)

            def flatten_values(b):
                pe.wait_ge(v_part, 3 * (b + 1))
                for j in range(CH):
                    s = P * j % K2
                    h = first_head[j]
                    for n in range(3):
                        m = pe.matmul(psA[:, j * 3 * HD:(j + 1) * 3 * HD], pick_key[:, s:s + P], vparts[:, n, h * HD:(h + 3) * HD], start=(n == 0), stop=(n == 2))
                m.then_inc(v_ps, 1)

            def scores(i, u, t, b):
                pe.wait_ge(q_lo, DC * (b + 1))
                pe.wait_ge(kbd_done, 2 * DC * (b + 1))
                pe.wait_ge(mrow_done, b + 1)
                if known(i, 1):
                    pe.wait_ge(s_sub, i)
                    pe.wait_ge(s_heads, (H - S_FULL * HB) * i)
                for n, h, k in S_BANKS:
                    pe.matmul(psS[:, n, 0:k * K2], share[:], mrow[:, u].rearrange("p (o k) -> p o k", o=1).to_broadcast([P, k, K2]),
                              start=True, stop=False, skip_group_check=True)
                for (q_part, k_part), (n, c, h0, h1) in ((part, piece) for part in PARTS for piece in S_PIECES):
                    first = S_BANKS[n][1]
                    m = pe.matmul(psS[:, n, (h0 - first) * K2:(h1 - first) * K2], qT[:, u, q_part, c, t * P:(t + 1) * P],
                                  kbd[:, u, k_part, c, h0 - c * HC:h1 - c * HC].rearrange("p h k -> p (h k)"),
                                  start=False, stop=True, skip_group_check=True)
                m.then_inc(s_ps, 1)

            def prob_T(i, t, g):
                c0, c1 = T_GROUPS[g]
                if g == 0:
                    pe.wait_ge(p_done, i + 1)
                if known(3 * i + g, 1):
                    pe.wait_ge(t_sb, 3 * i + g)
                for c in range(c0, c1):
                    m = pe.transpose(psT[:, (c - c0) * P:(c - c0 + 1) * P], prob[:, t, c * P:(c + 1) * P], ident[:])
                m.then_inc(t_ps, 1)

            def attend(i, u, b, g):
                pe.wait_ge(t_sb, 3 * i + g + 1)
                if g == 0:
                    pe.wait_ge(v_sb, b + 1)
                    if known(i, 1):
                        pe.wait_ge(o_sb, i)
                for c in range(*T_GROUPS[g]):
                    h = first_head[c]
                    m = pe.matmul(psB[:, h * VW:(h + 3) * VW], probT[:, c], vbd[:, u, c].rearrange("p h d -> p (h d)"),
                                  start=(c == 0), stop=(c == CH - 1), skip_group_check=True)
                if g == 2:
                    m.then_inc(o_ps, 1)

            def o_T(i):
                pe.wait_ge(o_sb, i + 1)
                if known(i, 1):
                    pe.wait_ge(x1_done, i)
                for c in range(DC):
                    m = pe.transpose(psY[:, c * P:(c + 1) * P], on[:, c * P:(c + 1) * P], ident[:])
                m.then_inc(oT_ps, 1)

            def project(i):
                pe.wait_ge(oT_sb, DC * (i + 1))
                for c in range(DC):
                    m = pe.matmul(psY, onT[:, c], wT["wfc"][:, c], start=(c == 0), stop=(c == DC - 1))
                m.then_inc(y_ps, 1)

            def n2_T(i, u4):
                pe.wait_ge(xn2_done, i + 1)
                if known(i, 1):
                    pe.wait_ge(base_done, i)
                for c in range(DC):
                    m = pe.transpose(psG[:, c * P:(c + 1) * P], rows[:, u4, 0, c * P:(c + 1) * P], ident[:])
                m.then_inc(n2T_ps, 1)

            def gate(i):
                pe.wait_ge(n2T_sb, i + 1)
                for c in range(DC):
                    m = pe.matmul(psG[:, D:D + E], xn2T[:, c], gate_sb[:, c], start=(c == 0), stop=(c == DC - 1))
                m.then_inc(g_ps, 1)

            def rank(i):
                pe.wait_ge(l_any, i + 1)
                pe.matmul(psG[:, D + E:D + 2 * E], upper[:], chosen_any[:], start=True, stop=True)
                pe.matmul(psG[:, D + 2 * E:D + 3 * E], ones[:], chosen_any[:], start=True, stop=True).then_inc(r_ps, 1)

            pe.wait_ge(wT_sb, 4)
            ctx_T(0, 0, 0)
            x_T(0)
            keys(0)
            queries(0, 0)
            queries(0, 1)
            values(0)
            pe.wait_ge(dv_const, 2)
            pe.wait_ge(gate_in, 16)
            flatten_values(0)
            ctx_T(1, 1, 0)
            scores(0, 0, 0, 0)
            keys(1)
            x_T(1)
            prob_T(0, 0, 0)
            scores(1, 0, 1, 0)

            def batch(b, u, n):
                more, more2 = below(b, B - 1), below(b, B - 2)
                for t in range(QT):
                    i = b * QT + t
                    u4 = u * QT + t
                    prob_T(i, t, 1)
                    if t == 0 and more:
                        queries(b + 1, 0)
                    if t == 0:
                        if more:
                            pe.wait_ge(k_raw, DC * (b + 2))
                    elif more2:
                        pe.wait_ge(ctxT_sb, b + 3)
                    if known(i, 1):
                        o_T(i - 1)
                    if known(i, 3):
                        rank(i - 3)
                    if t == 0 and more:
                        queries(b + 1, 1)
                    attend(i, u, b, 0)
                    prob_T(i, t, 2)
                    attend(i, u, b, 1)
                    attend(i, u, b, 2)
                    if known(i, 2):
                        n2_T(i - 2, (u4 - 2) % 4)
                    if t == 1 and more:
                        flatten_values(b + 1)
                    if known(i, 1):
                        project(i - 1)
                    if known(i, 2):
                        gate(i - 2)
                    if t == 1 and more2:
                        x_T(b + 2)
                    if t == 0 and more:
                        values(b + 1)
                    if t == 0 or more:
                        prob_T(i + 1, 1 - t, 0)
                    if more:
                        scores(i + 2, 1 - u, t, b + 1)
                    if more2:
                        if known(i, 1):
                            pe.wait_ge(x1_done, i)
                        if t == 0:
                            ctx_T(b + 2, u, n + 1)
                        else:
                            keys(b + 2)

            batches(pe, batch)
            o_T(NT - 1)
            rank(NT - 3)
            project(NT - 1)
            n2_T(NT - 2, 2)
            gate(NT - 2)
            rank(NT - 2)
            n2_T(NT - 1, 3)
            gate(NT - 1)
            rank(NT - 1)

            pe.wait_ge(tab_done, 1)

            def e_T(t, u, h):
                pe.wait_ge(et_in[u % 2], 16 * (h + 1))
                if known(t, 1):
                    pe.wait_ge(etT_lo, t)
                for c in range(DC):
                    m = pe.transpose(psG[:, c * P:(c + 1) * P], et[:, u % 2, c * P:(c + 1) * P], ident[:])
                m.then_inc(etT_ps, 1)

            w_of = w_all[:].rearrange("p (e c) s r f -> p e (c s r f)", c=DC)

            def weight(e, c, part, run, first=0, n=F):
                at = ((c * 2 + part) * FR + run) * F + first
                return w_of[:, bass.ds(e, 1), at:at + n].rearrange("p o f -> p (o f)")

            def up(t, u, e, n, bank, done):
                steps = [(a, w, c) for a, w in PARTS for c in range(DC)]
                for j, (a, w, c) in enumerate(steps):
                    if n == 0 and (a, c) == (1, 0):
                        pe.wait_ge(etT_lo, t + 1)
                    m = pe.matmul(banks4[:, bank], etT[:, u % 2, a, c], weight(e, c, w, n), start=(j == 0), stop=(j == len(steps) - 1))
                m.then_inc(done, 1)

            def g_T(t):
                pe.wait_ge(hg_done, t + 1)
                if known(t, 1):
                    pe.wait_ge(hgT_lo, t)
                for c in range(FC):
                    m = pe.transpose(psT[:, c * P:(c + 1) * P], hs[:, c * P:(c + 1) * P], ident[:])
                m.then_inc(hgT_ps, 1)

            def down(t, e):
                pe.wait_ge(hgT_hi, t + 1)
                if known(t, 1):
                    pe.wait_ge(ey_done, t)
                steps = [(a, w, c) for a, w in PARTS for c in range(FC)]
                for j, (a, w, c) in enumerate(steps):
                    if (a, c) == (1, 0):
                        pe.wait_ge(hgT_lo, t + 1)
                    m = pe.matmul(psB[:, 0:D], hgT[:, a, c], weight(e, c // 2, w, 2, c % 2 * D, D), start=(j == 0), stop=(j == len(steps) - 1))
                m.then_inc(ey_ps, 1)

            def expert_with_weights(t):
                e = pe.value_load(texp_i[0:1, bass.ds(t, 1)], min_val=0, max_val=E - 1)
                pe.wait_ge(w_in, (e + 1) * (DC * 2 * 16))
                return e

            e_T(0, 0, 0)
            expert = {}
            next_expert, last_expert = pe.alloc_register("next_expert"), pe.alloc_register("last_expert")

            def tile(t, u, q):
                if u == 0:
                    if known(t, 1):
                        expert[0], expert[-1] = (pe.snap(r, min_val=0, max_val=E - 1) for r in (next_expert, last_expert))
                    else:
                        expert[0] = expert_with_weights(t)
                pe.wait_ge(etT_hi, t + 1)
                if known(t, 2):
                    pe.wait_ge(hg_done, t - 1)
                up(t, u, expert[u], 0, u % 2, h0_ps)
                if below(t, MOE_T - 1):
                    expert[u + 1] = expert_with_weights(t + 1)
                    if u == UNROLL - 1:
                        pe.reg_mov(next_expert, expert[u + 1])
                        pe.reg_mov(last_expert, expert[u])
                if known(t, 1):
                    g_T(t - 1)
                if below(t, MOE_T - 1):
                    e_T(t + 1, u + 1, (q * UNROLL + u + 1) // 2 if isinstance(q, int) else q * (UNROLL // 2) + (u + 1) // 2)
                up(t, u, expert[u], 1, 2 + u % 2, h1_ps)
                if known(t, 1):
                    down(t - 1, expert[u - 1])

            UNROLL = 8
            tiles(pe, tile, unroll=UNROLL)
            g_T(MOE_T - 1)
            down(MOE_T - 1, expert[(MOE_T - 1) % UNROLL])


_INS = ["x", "ctx_1024", "mask_BxS2_ik0", "g_xattn", "g_ffn",
        "L0_xattn_Wq", "L0_xattn_bq", "L0_xattn_Wk", "L0_xattn_bk", "L0_xattn_Wv", "L0_xattn_bv",
        "L0_xattn_Wfc", "L0_xattn_bfc", "L0_ffn_gate_kernel", "L0_ffn_w0_kernel", "L0_ffn_w1_kernel",
        "L0_ffn_wo_kernel"]


def kernel(**inputs):
    import numpy as _np
    import concourse.bacc as _bacc
    from concourse import mybir as _mybir
    from concourse.bass_utils import run_bass_kernel_spmd as _run

    nc = _bacc.Bacc("TRN2", target_bir_lowering=False, num_devices=1)
    arrays, args = {}, []
    for name in _INS:
        a = _np.ascontiguousarray(inputs[name])
        arrays[f"in_{name}_dram"] = a
        args.append(nc.dram_tensor(f"in_{name}_dram", a.shape, _mybir.dt.from_np(a.dtype), kind="ExternalInput").ap())
    B, S, D = inputs["x"].shape
    args.append(nc.dram_tensor("out_0_dram", (B * S + P, D), F32, kind="ExternalOutput").ap())
    flamingo_gated_layer(nc, *args)
    r = _run(nc, [arrays], core_ids=[0])
    return r.results[0]["out_0_dram"][:B * S].reshape(B, S, D)
```
